# Optimizing a Trainium2 kernel written in Bass

```python
import numpy as np
import jax
import jax.numpy as jnp

def _softmax(x, axis=-1):
    return jax.nn.softmax(x, axis=axis)

def _gelu(x):
    return jax.nn.gelu(x, approximate=True)

def _silu(x):
    return jax.nn.silu(x)

def _sigmoid(x):
    return jax.nn.sigmoid(x)

def _layernorm(x, axis=-1, eps=1e-05):
    m = jnp.mean(x, axis=axis, keepdims=True)
    v = jnp.var(x, axis=axis, keepdims=True)
    return (x - m) / jnp.sqrt(v + eps)

def _scatter_add(tgt, idx, src, axis=0):
    return tgt.at[idx].add(src)

def _segment_sum(src, seg, n):
    return jax.ops.segment_sum(src, seg, n)
kernel_name = 'mk_dlrm_tower_d1_rec_r8_4526d2'

def setup_inputs(seed: int=0):
    np.random.seed(seed)
    _w = jnp.asarray

    def _rec_inputs():
        import jax
        import jax.numpy as jnp
        _tk = jax.random.key(seed)
        dense_ctx = jax.random.normal(jax.random.fold_in(_tk, 190), (512, 16), jnp.float32)
        ids = jnp.stack([jax.random.randint(jax.random.fold_in(_tk, 200 + f), (512,), 0, v, jnp.int32) for f, v in enumerate([1250, 1250, 1250, 125000, 12500, 1250, 1000, 12500, 1250, 1000, 1250, 125000, 125000, 1250, 1250, 1000, 125000, 125000, 1250, 1000, 1250, 1000, 1000, 12500, 125000, 1250, 12500, 1250, 125000, 1000, 1000, 1250])], axis=1)
        tbl_0 = 0.05 * jax.random.normal(jax.random.fold_in(_tk, 500 + 0), (1250, 32), jnp.float32)
        tbl_1 = 0.05 * jax.random.normal(jax.random.fold_in(_tk, 500 + 1), (1250, 32), jnp.float32)
        tbl_2 = 0.05 * jax.random.normal(jax.random.fold_in(_tk, 500 + 2), (1250, 32), jnp.float32)
        tbl_3 = 0.05 * jax.random.normal(jax.random.fold_in(_tk, 500 + 3), (125000, 32), jnp.float32)
        tbl_4 = 0.05 * jax.random.normal(jax.random.fold_in(_tk, 500 + 4), (12500, 32), jnp.float32)
        tbl_5 = 0.05 * jax.random.normal(jax.random.fold_in(_tk, 500 + 5), (1250, 32), jnp.float32)
        tbl_6 = 0.05 * jax.random.normal(jax.random.fold_in(_tk, 500 + 6), (1000, 32), jnp.float32)
        tbl_7 = 0.05 * jax.random.normal(jax.random.fold_in(_tk, 500 + 7), (12500, 32), jnp.float32)
        tbl_8 = 0.05 * jax.random.normal(jax.random.fold_in(_tk, 500 + 8), (1250, 32), jnp.float32)
        tbl_9 = 0.05 * jax.random.normal(jax.random.fold_in(_tk, 500 + 9), (1000, 32), jnp.float32)
        tbl_10 = 0.05 * jax.random.normal(jax.random.fold_in(_tk, 500 + 10), (1250, 32), jnp.float32)
        tbl_11 = 0.05 * jax.random.normal(jax.random.fold_in(_tk, 500 + 11), (125000, 32), jnp.float32)
        tbl_12 = 0.05 * jax.random.normal(jax.random.fold_in(_tk, 500 + 12), (125000, 32), jnp.float32)
        tbl_13 = 0.05 * jax.random.normal(jax.random.fold_in(_tk, 500 + 13), (1250, 32), jnp.float32)
        tbl_14 = 0.05 * jax.random.normal(jax.random.fold_in(_tk, 500 + 14), (1250, 32), jnp.float32)
        tbl_15 = 0.05 * jax.random.normal(jax.random.fold_in(_tk, 500 + 15), (1000, 32), jnp.float32)
        tbl_16 = 0.05 * jax.random.normal(jax.random.fold_in(_tk, 500 + 16), (125000, 32), jnp.float32)
        tbl_17 = 0.05 * jax.random.normal(jax.random.fold_in(_tk, 500 + 17), (125000, 32), jnp.float32)
        tbl_18 = 0.05 * jax.random.normal(jax.random.fold_in(_tk, 500 + 18), (1250, 32), jnp.float32)
        tbl_19 = 0.05 * jax.random.normal(jax.random.fold_in(_tk, 500 + 19), (1000, 32), jnp.float32)
        tbl_20 = 0.05 * jax.random.normal(jax.random.fold_in(_tk, 500 + 20), (1250, 32), jnp.float32)
        tbl_21 = 0.05 * jax.random.normal(jax.random.fold_in(_tk, 500 + 21), (1000, 32), jnp.float32)
        tbl_22 = 0.05 * jax.random.normal(jax.random.fold_in(_tk, 500 + 22), (1000, 32), jnp.float32)
        tbl_23 = 0.05 * jax.random.normal(jax.random.fold_in(_tk, 500 + 23), (12500, 32), jnp.float32)
        tbl_24 = 0.05 * jax.random.normal(jax.random.fold_in(_tk, 500 + 24), (125000, 32), jnp.float32)
        tbl_25 = 0.05 * jax.random.normal(jax.random.fold_in(_tk, 500 + 25), (1250, 32), jnp.float32)
        tbl_26 = 0.05 * jax.random.normal(jax.random.fold_in(_tk, 500 + 26), (12500, 32), jnp.float32)
        tbl_27 = 0.05 * jax.random.normal(jax.random.fold_in(_tk, 500 + 27), (1250, 32), jnp.float32)
        tbl_28 = 0.05 * jax.random.normal(jax.random.fold_in(_tk, 500 + 28), (125000, 32), jnp.float32)
        tbl_29 = 0.05 * jax.random.normal(jax.random.fold_in(_tk, 500 + 29), (1000, 32), jnp.float32)
        tbl_30 = 0.05 * jax.random.normal(jax.random.fold_in(_tk, 500 + 30), (1000, 32), jnp.float32)
        tbl_31 = 0.05 * jax.random.normal(jax.random.fold_in(_tk, 500 + 31), (1250, 32), jnp.float32)
        _rk = jax.random.fold_in(_tk, 7)
        W_top1 = 0.0606339 * jax.random.normal(jax.random.fold_in(_tk, 801), (272, 512), jnp.float32)
        W_top2 = 0.0441942 * jax.random.normal(jax.random.fold_in(_tk, 802), (512, 256), jnp.float32)
        W_top3 = 0.0625 * jax.random.normal(jax.random.fold_in(_tk, 803), (256, 1), jnp.float32)
        b_top1 = jnp.zeros((512,), jnp.float32)
        b_top2 = jnp.zeros((256,), jnp.float32)
        return (dense_ctx, ids, tbl_0, tbl_1, tbl_2, tbl_3, tbl_4, tbl_5, tbl_6, tbl_7, tbl_8, tbl_9, tbl_10, tbl_11, tbl_12, tbl_13, tbl_14, tbl_15, tbl_16, tbl_17, tbl_18, tbl_19, tbl_20, tbl_21, tbl_22, tbl_23, tbl_24, tbl_25, tbl_26, tbl_27, tbl_28, tbl_29, tbl_30, tbl_31, W_top1, b_top1, W_top2, b_top2, W_top3)
    dense_ctx, ids, tbl_0, tbl_1, tbl_2, tbl_3, tbl_4, tbl_5, tbl_6, tbl_7, tbl_8, tbl_9, tbl_10, tbl_11, tbl_12, tbl_13, tbl_14, tbl_15, tbl_16, tbl_17, tbl_18, tbl_19, tbl_20, tbl_21, tbl_22, tbl_23, tbl_24, tbl_25, tbl_26, tbl_27, tbl_28, tbl_29, tbl_30, tbl_31, W_top1, b_top1, W_top2, b_top2, W_top3 = _rec_inputs()

    def _L0_rec_setup():
        import jax, jax.numpy as jnp
        import numpy as np
        B, F, D = (512, 32, 32)
        LAYER_SIZE = [128, 128]

        def _cin_forward(inputs, filters):
            x0 = inputs
            prev = inputs
            outs = []
            for W in filters:
                z = jnp.einsum('bhd,bmd->bhmd', x0, prev)
                b, h, m, d = z.shape
                z = z.reshape(b, h * m, d)
                cur = jnp.einsum('bpd,pn->bnd', z, W[0])
                cur = jax.nn.relu(cur)
                prev = cur
                outs.append(cur)
            result = jnp.concatenate(outs, axis=1)
            return jnp.sum(result, axis=-1)
        key = jax.random.key(seed)
        k1, k2, k3 = jax.random.split(key, 3)
        inputs = jax.random.normal(k1, (B, F, D), dtype=jnp.float32)
        field_nums = [F] + LAYER_SIZE
        filter_0 = jax.random.normal(k2, (1, field_nums[0] * field_nums[0], field_nums[1]), dtype=jnp.float32) * 0.05
        filter_1 = jax.random.normal(k3, (1, field_nums[0] * field_nums[1], field_nums[2]), dtype=jnp.float32) * 0.05
        return {'inputs': inputs, 'filter_0': filter_0, 'filter_1': filter_1}
    _L0_rec_all = _L0_rec_setup()
    _L0_rec_in = {k: v for k, v in _L0_rec_all.items() if k in ('filter_0', 'filter_1')}
    del _L0_rec_all
    return {'dense_ctx': dense_ctx, 'ids': ids, 'tbl_0': tbl_0, 'tbl_1': tbl_1, 'tbl_2': tbl_2, 'tbl_3': tbl_3, 'tbl_4': tbl_4, 'tbl_5': tbl_5, 'tbl_6': tbl_6, 'tbl_7': tbl_7, 'tbl_8': tbl_8, 'tbl_9': tbl_9, 'tbl_10': tbl_10, 'tbl_11': tbl_11, 'tbl_12': tbl_12, 'tbl_13': tbl_13, 'tbl_14': tbl_14, 'tbl_15': tbl_15, 'tbl_16': tbl_16, 'tbl_17': tbl_17, 'tbl_18': tbl_18, 'tbl_19': tbl_19, 'tbl_20': tbl_20, 'tbl_21': tbl_21, 'tbl_22': tbl_22, 'tbl_23': tbl_23, 'tbl_24': tbl_24, 'tbl_25': tbl_25, 'tbl_26': tbl_26, 'tbl_27': tbl_27, 'tbl_28': tbl_28, 'tbl_29': tbl_29, 'tbl_30': tbl_30, 'tbl_31': tbl_31, 'W_top1': W_top1, 'b_top1': b_top1, 'W_top2': W_top2, 'b_top2': b_top2, 'W_top3': W_top3, 'L0_rec_filter_0': _L0_rec_in['filter_0'], 'L0_rec_filter_1': _L0_rec_in['filter_1']}

def reference(dense_ctx, ids, tbl_0, tbl_1, tbl_2, tbl_3, tbl_4, tbl_5, tbl_6, tbl_7, tbl_8, tbl_9, tbl_10, tbl_11, tbl_12, tbl_13, tbl_14, tbl_15, tbl_16, tbl_17, tbl_18, tbl_19, tbl_20, tbl_21, tbl_22, tbl_23, tbl_24, tbl_25, tbl_26, tbl_27, tbl_28, tbl_29, tbl_30, tbl_31, W_top1, b_top1, W_top2, b_top2, W_top3, L0_rec_filter_0, L0_rec_filter_1):
    import jax
    import jax.numpy as jnp

    def _L0_rec_ref(inputs, filter_0, filter_1):
        import jax, jax.numpy as jnp
        import numpy as np
        B, F, D = (512, 32, 32)
        LAYER_SIZE = [128, 128]

        def _cin_forward(inputs, filters):
            x0 = inputs
            prev = inputs
            outs = []
            for W in filters:
                z = jnp.einsum('bhd,bmd->bhmd', x0, prev)
                b, h, m, d = z.shape
                z = z.reshape(b, h * m, d)
                cur = jnp.einsum('bpd,pn->bnd', z, W[0])
                cur = jax.nn.relu(cur)
                prev = cur
                outs.append(cur)
            result = jnp.concatenate(outs, axis=1)
            return jnp.sum(result, axis=-1)
        return _cin_forward(inputs, (filter_0, filter_1))
    e = jnp.stack([tbl_0[ids[:, 0]], tbl_1[ids[:, 1]], tbl_2[ids[:, 2]], tbl_3[ids[:, 3]], tbl_4[ids[:, 4]], tbl_5[ids[:, 5]], tbl_6[ids[:, 6]], tbl_7[ids[:, 7]], tbl_8[ids[:, 8]], tbl_9[ids[:, 9]], tbl_10[ids[:, 10]], tbl_11[ids[:, 11]], tbl_12[ids[:, 12]], tbl_13[ids[:, 13]], tbl_14[ids[:, 14]], tbl_15[ids[:, 15]], tbl_16[ids[:, 16]], tbl_17[ids[:, 17]], tbl_18[ids[:, 18]], tbl_19[ids[:, 19]], tbl_20[ids[:, 20]], tbl_21[ids[:, 21]], tbl_22[ids[:, 22]], tbl_23[ids[:, 23]], tbl_24[ids[:, 24]], tbl_25[ids[:, 25]], tbl_26[ids[:, 26]], tbl_27[ids[:, 27]], tbl_28[ids[:, 28]], tbl_29[ids[:, 29]], tbl_30[ids[:, 30]], tbl_31[ids[:, 31]]], axis=1)
    z = _L0_rec_ref(e, L0_rec_filter_0, L0_rec_filter_1)
    z = z.reshape(z.shape[0], -1)
    h = jnp.concatenate([z, dense_ctx], axis=1)
    h = jnp.maximum(h @ W_top1 + b_top1, 0.0)
    h = jnp.maximum(h @ W_top2 + b_top2, 0.0)
    y = h @ W_top3
    return y

_drawn_inputs = setup_inputs


def setup_inputs(seed=0):
    import zlib

    import numpy as np

    out = dict(_drawn_inputs(seed))
    spreads = {'b_top1': (0.0, 0.434), 'b_top2': (0.0, 0.426)}
    factors = {'tbl_0': 5.709,
     'tbl_1': 5.84,
     'tbl_2': 6.189,
     'tbl_3': 6.211,
     'tbl_4': 6.016,
     'tbl_5': 6.276,
     'tbl_6': 6.188,
     'tbl_7': 6.057,
     'tbl_8': 6.33,
     'tbl_9': 6.243,
     'tbl_10': 6.15,
     'tbl_11': 6.113,
     'tbl_12': 5.749,
     'tbl_13': 5.864,
     'tbl_14': 6.012,
     'tbl_15': 5.924,
     'tbl_16': 6.058,
     'tbl_17': 5.805,
     'tbl_18': 6.317,
     'tbl_19': 5.926,
     'tbl_20': 5.99,
     'tbl_21': 6.162,
     'tbl_22': 5.88,
     'tbl_23': 6.3,
     'tbl_24': 5.913,
     'tbl_25': 5.754,
     'tbl_26': 5.852,
     'tbl_27': 5.961,
     'tbl_28': 6.166,
     'tbl_29': 6.266,
     'tbl_30': 6.122,
     'tbl_31': 5.915,
     'L0_rec_filter_1': 8.0}
    for name, (base, spread) in spreads.items():
        noise = np.random.default_rng([zlib.crc32(name.encode()), seed]).standard_normal(out[name].shape)
        drawn = base * np.exp(spread * noise) if base else spread * noise
        out[name] = jnp.asarray(drawn.astype(out[name].dtype))
    for name, factor in factors.items():
        out[name] = (out[name] * factor).astype(out[name].dtype)
    return out
```

```python
import numpy as np
import concourse.bass as bass
from concourse import mybir
from contextlib import ExitStack

P = 128
BATCH, FIELDS, COLS, FEATS = 512, 32, 32, 128
BT = BATCH // P
J = 4
UPT = COLS // J
UNITS = BT * UPT
W = J * P
REP = P // FIELDS
CHUNKS = (FIELDS // 2) // REP
HB = 4
SPT = FIELDS // HB
STEPS = J * SPT
SUMS = 2
YB = 6
TR = 2 * J
ROWS = SPT // 2 * HB
MLP1, MLP2, DENSE = 512, 256, 16

AT_PERMUTE, AT_TRANSPOSE, AT_EVACUATE = 1, 4, 6
AT_FINISH, AT_PRODUCTS, AT_LAYER1 = 11, 16, 18
AT_HI5, AT_LO5, AT_HI, AT_LO = 22, 22, 26, 27
GATHERS = [5, 5, 5, 5, 4, 4, 4, 0]

MAC0, SCALED0, SUMS0, FINISHED0 = YB // 2 * HB, YB // 2, TR, 1
LOADS = REP + 1 + 1


def bank_before(q):
    n = UPT * STEPS
    return q - YB if q >= YB else max(x for x in range(n - YB, n) if x % YB == q) - n


def tower(nc, ids, tables, w1a, w1b, w1s, f1, eye, dense_t, wt1, bt1, wt2, bt2, wt3, out):
    f32, f32r, i32 = mybir.dt.float32, mybir.dt.float32r, mybir.dt.int32
    ALU, ACT, AX = mybir.AluOpType, mybir.ActivationFunctionType, mybir.AxisListType
    ctx = ExitStack()
    with ctx:
        def sb(name, shape, dt=f32):
            return ctx.enter_context(nc.sbuf_tensor(name, shape, dt))

        def sem(name):
            return ctx.enter_context(nc.semaphore(name))

        ids_all = sb("ids_all", [P, BT, FIELDS], i32)
        ids_next = sb("ids_next", [P, FIELDS], i32)
        rows = sb("rows", [P, FIELDS, COLS])
        x = sb("x", [P, UPT, J, FIELDS])
        ident = sb("ident", [P, P])
        xt = sb("xt", [P, P])
        xt_dram = nc.dram_tensor("xt_dram", (2 * FIELDS, J, P), f32, kind="Internal").ap()
        fa = sb("fa", [P, CHUNKS, FEATS])
        fb = sb("fb", [P, CHUNKS, FEATS])
        f0 = sb("f0", [P, CHUNKS, FEATS])
        f0s = sb("f0s", [P, FEATS])
        f0p = sb("f0p", [P, FEATS], f32r)
        a_rows = sb("a_rows", [P, W])
        b_rows = sb("b_rows", [P, CHUNKS, W])
        bs_rows = sb("bs_rows", [P, W])
        z = sb("z", [P, CHUNKS, W])
        zs = sb("zs", [P, W])
        zp = sb("zp", [P, W], f32r)
        f1_hi = sb("f1_hi", [P, FIELDS * FEATS], f32r)
        f1_lo = sb("f1_lo", [P, FIELDS * FEATS], f32r)
        cur_hi = sb("cur_hi", [P, 2, W], f32r)
        cur_lo = sb("cur_lo", [P, 2, W], f32r)
        acc = sb("acc", [P, 2, SUMS, J, FEATS])
        scaled = sb("scaled", [P, TR, ROWS, FEATS])
        sums = sb("sums", [P, 2, J, FEATS])
        total = sb("total", [P, J, FEATS])
        f1_raw = scaled[:, 0:2, :, :].rearrange("p t r n -> p (t r n)")
        z1 = sb("z1", [P, J, P])
        z2 = sb("z2", [P, J, FEATS])
        z1_all = sb("z1_all", [P, BT * P])
        z2_all = sb("z2_all", [P, BT + 1, FEATS])
        z2_t = sb("z2_t", [P, BATCH])
        dense_sb = sb("dense_sb", [DENSE, BATCH])
        wt1_sb = sb("wt1_sb", [P, 2, MLP1])
        wt1_d = sb("wt1_d", [DENSE, MLP1])
        wt2_sb = sb("wt2_sb", [P, MLP1 // P, MLP2])
        wt3_sb = sb("wt3_sb", [P, MLP2 // P])
        bt1_sb = sb("bt1_sb", [P, MLP1 // P])
        bt2_sb = sb("bt2_sb", [P, MLP2 // P])
        h1 = scaled[:, 0, :, :].rearrange("p r n -> p (r n)")
        h2 = scaled[:, 1, 0:8, :].rearrange("p r n -> p (r n)")
        y_row = sb("y_row", [1, BATCH])

        y_ps = [ctx.enter_context(nc.psum_tensor(f"y_ps{i}", [P, HB, FEATS], f32)) for i in range(YB)]
        cur_ps = ctx.enter_context(nc.psum_tensor("cur_ps", [P, W], f32))
        xt_ps = ctx.enter_context(nc.psum_tensor("xt_ps", [P, W], f32))

        ids_in = sem("ids_in")
        eye_in = sem("eye_in")
        f0_in = sem("f0_in")
        f1_in = sem("f1_in")
        mlp_in = sem("mlp_in")
        f0_folded = sem("f0_folded")
        f0_parted = sem("f0_parted")
        f1_hi_done = sem("f1_hi_done")
        f1_split = sem("f1_split")
        ids_staged = sem("ids_staged")
        gathered = sem("gathered")
        permuted = sem("permuted")
        transposed = sem("transposed")
        xt_ready = sem("xt_ready")
        xt_stored = sem("xt_stored")
        ab_loaded = sem("ab_loaded")
        products = sem("products")
        hi5_done = sem("hi5_done")
        lo5_done = sem("lo5_done")
        cur_done = sem("cur_done")
        hi_done = sem("hi_done")
        lo_done = sem("lo_done")
        z1_added = sem("z1_added")
        z1_reduced = sem("z1_reduced")
        y_ready = sem("y_ready")
        macs = sem("macs")
        scaled_done = sem("scaled_done")
        pool_chain = sem("pool_chain")
        sums_done = sem("sums_done")
        finish_chain = sem("finish_chain")
        finished = sem("finished")
        z2_reduced = sem("z2_reduced")
        cleared = sem("cleared")
        z2t_ready = sem("z2t_ready")
        z2t_copied = sem("z2t_copied")
        h1_ready = sem("h1_ready")
        h1_done = sem("h1_done")
        h2_ready = sem("h2_ready")
        h2_done = sem("h2_done")
        row_ready = sem("row_ready")
        row_copied = sem("row_copied")
        out_stored = sem("out_stored")

        block = ctx.enter_context(nc.Block())

        def batch_tiles(engine, body):
            with engine.Fori(0, BT - 1) as t:
                body(t, False)
            body(BT - 1, True)

        @block.sync
        def _(sp):
            sp.dma_start(ids_all[:, :, :], ids.rearrange("(t p) f -> p t f", p=P)).then_inc(ids_in, 16)
            sp.dma_start(ident[:, :], eye).then_inc(eye_in, 16)
            sp.dma_start(fa[:, :, :], w1a).then_inc(f0_in, 16)
            sp.dma_start(fb[:, :, :], w1b).then_inc(f0_in, 16)
            sp.dma_start(f0s[:, :], w1s).then_inc(f0_in, 16)
            sp.dma_start(f1_raw.rearrange("m (h n) -> m h n", n=FEATS),
                         f1.rearrange("(h m) n -> m h n", m=FEATS)).then_inc(f1_in, 16)
            sp.dma_start(wt1_sb[:, :, :], wt1[0:2 * P, :].rearrange("(k p) n -> p k n", p=P)).then_inc(mlp_in, 16)
            sp.dma_start(wt1_d[:, :], wt1[2 * P:2 * P + DENSE, :]).then_inc(mlp_in, 16)
            sp.dma_start(wt2_sb[:, :, :], wt2.rearrange("(k p) n -> p k n", p=P)).then_inc(mlp_in, 16)
            sp.dma_start(wt3_sb[:, :], wt3).then_inc(mlp_in, 16)
            sp.dma_start(bt1_sb[:, :], bt1).then_inc(mlp_in, 16)
            sp.dma_start(bt2_sb[:, :], bt2).then_inc(mlp_in, 16)
            sp.dma_start(dense_sb[:, :], dense_t).then_inc(mlp_in, 16)

            def spread(unit):
                first = isinstance(unit, int)
                here, stored, read, made = [v if first else sp.to_reg(v) for v in (
                    unit + 1, unit * (16 * 2 * J) + 16 * 2 * J, unit * (16 * LOADS), unit * (CHUNKS + 1))]
                if not first:
                    sp.wait_ge(ab_loaded, read)
                sp.wait_ge(xt_ready, here)
                for half in range(2):
                    for j in range(J):
                        sp.dma_start(xt_dram[half * FIELDS:(half + 1) * FIELDS, j, :],
                                     xt[j * FIELDS:(j + 1) * FIELDS, :]).then_inc(xt_stored, 16)
                if not first:
                    sp.wait_ge(products, made)
                sp.wait_ge(xt_stored, stored)
                for r in range(REP):
                    part = slice(r * FIELDS, (r + 1) * FIELDS)
                    src = xt_dram[r:r + FIELDS, :, :]
                    rotated = bass.AP(src.tensor, src.offset, [[W, FIELDS], [REP * W, CHUNKS], [1, W]])
                    sp.dma_start(b_rows[part, :, :], rotated).then_inc(ab_loaded, 16)
                for dst, at in ((a_rows, 0), (bs_rows, FIELDS // 2)):
                    src = xt_dram[at:at + FIELDS, :, :]
                    repeated = bass.AP(src.tensor, src.offset, [[0, REP], [W, FIELDS], [1, W]])
                    sp.dma_start(dst[:, :], repeated).then_inc(ab_loaded, 16)

            spread(0)
            with sp.Fori(1, UNITS) as unit:
                spread(unit)
            sp.wait_ge(row_copied, 1)
            sp.dma_start(out.rearrange("b o -> o b"), y_row[:, :]).then_inc(out_stored, 16)
            sp.wait_ge(out_stored, 16)

        @block.gpsimd
        def _(pool):
            def gather(h, ids_tile):
                pool.indirect_dma_start(
                    out=rows[:, h, :], out_offset=None, in_=tables[h],
                    in_offset=bass.IndirectOffsetOnAxis(ap=ids_tile[:, h:h + 1], axis=0)).then_inc(gathered, 16)

            pool.wait_ge(ids_in, 16)
            for h in range(FIELDS):
                gather(h, ids_all[:, 0, :])
            nc.gpsimd.memset(sums[:, 1, :, :], 0.0).then_inc(sums_done, SUMS0)

            def add_up(unit, unit_even, j, staged=None):
                tile_no = unit * J + j
                ring = j if unit_even else J + j
                t = scaled[:, ring, :, :]
                if staged is not None:
                    pool.wait_ge(ids_staged, staged)
                pool.wait_ge(scaled_done, unit * (STEPS // 2) + (SCALED0 + (j + 1) * SPT // 2))
                n, k = ROWS // 2, 0
                while n >= 2:
                    nc.gpsimd.tensor_tensor(t[:, 0:n, :], t[:, 0:n, :], t[:, n:2 * n, :],
                                            ALU.add).then_inc(pool_chain, 1)
                    k += 1
                    pool.wait_ge(pool_chain, tile_no * 3 + k)
                    n //= 2
                if j == 0:
                    pool.wait_ge(finished, unit + 1)
                nc.gpsimd.tensor_tensor(sums[:, 0 if unit_even else 1, j, :], t[:, 0, :], t[:, 1, :],
                                        ALU.add).then_inc(sums_done, 1)

            def body(t, last):
                h = 0
                for u in range(UPT):
                    unit = t * UPT + u
                    if u == 0 and not last:
                        pool.wait_ge(permuted, t * 2 + 2)
                        nc.gpsimd.tensor_copy(ids_next[:, :], ids_all[:, t + 1, :]).then_inc(ids_staged, 1)
                    for j in range(J):
                        add_up(unit, u % 2 == 0, j, t + 1 if u == 0 and j == 0 and not last else None)
                        if not last:
                            for _ in range((GATHERS[u] + J - 1 - j) // J):
                                gather(h, ids_next)
                                h += 1

            batch_tiles(pool, body)

        @block.tensor
        def _(pe):
            def transpose(unit, dg, need):
                pe.wait_ge(permuted, need)
                pe.wait_ge(xt_ready, unit + 0) if not isinstance(unit, int) or unit > 0 else None
                nc.tensor.transpose(xt_ps[:, 0:P], x[:, dg, :, :], ident[:, :]).then_inc(transposed, 1)

            def layer1(unit, c, first=False):
                if c == 0 and not first:
                    pe.wait_ge(z1_added, unit)
                    pe.wait_ge(lo_done, unit)
                    pe.wait_ge(hi_done, unit)
                if c < CHUNKS:
                    pe.wait_ge(products, unit * (CHUNKS + 1) + (c + 1))
                    nc.tensor.matmul(cur_ps[:, :], f0[:, c, :], z[:, c, :], start=(c == 0), stop=False)
                else:
                    pe.wait_ge(lo5_done, unit + 1)
                    nc.tensor.matmul(cur_ps[:, :], f0p[:, :], zp[:, :], start=False, stop=True).then_inc(cur_done, 1)

            pe.wait_ge(eye_in, 16)
            transpose(0, 0, 1)
            pe.wait_ge(f0_folded, 2)
            pe.wait_ge(f0_parted, 3)
            for c in range(CHUNKS + 1):
                layer1(0, c, first=True)
            pe.wait_ge(f1_split, 1)

            def body(t, last):
                for u in range(UPT):
                    unit = t * UPT + u
                    look = not (last and u == UPT - 1)
                    for q in range(STEPS):
                        j, c = q // SPT, q % SPT
                        step = u * STEPS + q
                        if look and q == AT_TRANSPOSE:
                            need = t * 2 + (1 if u < UPT - 2 else 2 if u == UPT - 2 else 3)
                            transpose(unit + 1, (u + 1) % UPT, need)
                        if look and AT_LAYER1 <= q < AT_LAYER1 + CHUNKS:
                            layer1(unit + 1, q - AT_LAYER1)
                        if look and q == AT_LO5 + 2:
                            layer1(unit + 1, CHUNKS)
                        if q == 0:
                            pe.wait_ge(hi_done, unit + 1)
                            pe.wait_ge(lo_done, unit + 1)
                        before = bank_before(step)
                        if step % 2 == 0:
                            pe.wait_ge(macs, t * (UPT * STEPS // 2 * HB) + (MAC0 + before // 2 * HB + HB))
                        else:
                            pe.wait_ge(scaled_done, t * (UPT * STEPS // 2) + (SCALED0 + (before + 1) // 2))
                        bank = y_ps[step % YB][:, :, :].rearrange("p h n -> p (h n)")
                        cols = slice(c * W, (c + 1) * W)
                        hi = cur_hi[:, u % 2, j * P:(j + 1) * P]
                        lo = cur_lo[:, u % 2, j * P:(j + 1) * P]
                        nc.tensor.matmul(bank, hi, f1_hi[:, cols], start=True, stop=False)
                        nc.tensor.matmul(bank, hi, f1_lo[:, cols], start=False, stop=False)
                        nc.tensor.matmul(bank, lo, f1_hi[:, cols], start=False, stop=True).then_inc(y_ready, 1)

            batch_tiles(pe, body)

            pe.wait_ge(z2_reduced, BT + 1)
            pe.wait_ge(xt_ready, UNITS)
            for t in range(BT):
                last = nc.tensor.transpose(xt_ps[:, t * P:(t + 1) * P], z2_all[:, t + 1, :], ident[:, :])
            last.then_inc(z2t_ready, 1)
            pe.wait_ge(mlp_in, 16 * 7)
            pe.wait_ge(macs, MAC0 + HB * UNITS * STEPS // 2)
            pe.wait_ge(scaled_done, SCALED0 + UNITS * STEPS // 2)
            pe.wait_ge(z1_reduced, BT)
            flat = [b[:, :, :].rearrange("p h n -> p (h n)") for b in y_ps]
            for m in range(MLP1 // P):
                cols = slice(m * P, (m + 1) * P)
                nc.tensor.matmul(flat[m], wt1_sb[:, 0, cols], z1_all[:, :], start=True, stop=False)
                nc.tensor.matmul(flat[m], wt1_d[:, cols], dense_sb[:, :], start=False, stop=False)
            pe.wait_ge(z2t_copied, 1)
            for m in range(MLP1 // P):
                cols = slice(m * P, (m + 1) * P)
                nc.tensor.matmul(flat[m], wt1_sb[:, 1, cols], z2_t[:, :], start=False, stop=True).then_inc(h1_ready, 1)
            for k in range(MLP1 // P):
                pe.wait_ge(h1_done, k + 1)
                for m in range(MLP2 // P):
                    last = nc.tensor.matmul(flat[4 + m], wt2_sb[:, k, m * P:(m + 1) * P], h1[:, k * BATCH:(k + 1) * BATCH],
                                            start=(k == 0), stop=(k == MLP1 // P - 1))
            last.then_inc(h2_ready, 1)
            for k in range(MLP2 // P):
                pe.wait_ge(h2_done, k + 1)
                last = nc.tensor.matmul(cur_ps[0:1, :], wt3_sb[:, k:k + 1], h2[:, k * BATCH:(k + 1) * BATCH],
                                        start=(k == 0), stop=(k == MLP2 // P - 1))
            last.then_inc(row_ready, 1)

        @block.scalar
        def _(act):
            def evacuate(unit, first=False):
                act.wait_ge(transposed, unit + 1)
                if not first:
                    act.wait_ge(xt_stored, unit * (16 * 2 * J))
                nc.scalar.copy(xt[:, :], xt_ps[:, 0:P]).then_inc(xt_ready, 1)

            def hi5(unit):
                act.wait_ge(products, unit * (CHUNKS + 1) + (CHUNKS + 1))
                nc.scalar.copy(zp[:, :], zs[:, :]).then_inc(hi5_done, 1)

            def hi(unit, parity):
                act.wait_ge(cur_done, unit + 1)
                nc.scalar.activation(cur_hi[:, parity, :], cur_ps[:, :], ACT.Relu).then_inc(hi_done, 1)

            def permute(a, b):
                nc.scalar.copy(x[:, a:b, :, :].rearrange("p g j h -> p (g j) h"),
                               rows[:, :, a * J:b * J].rearrange("p h d -> p d h")).then_inc(permuted, 1)

            act.preload_act_table(ACT.Relu)
            act.sem_inc(scaled_done, SCALED0)
            act.wait_ge(f1_in, 16)
            nc.scalar.copy(f1_hi[:, :], f1_raw).then_inc(f1_hi_done, 1)
            act.wait_ge(gathered, 16 * FIELDS)
            permute(0, UPT - 1)
            evacuate(0, first=True)
            hi5(0)
            hi(0, 0)

            def body(t, last):
                for u in range(UPT):
                    unit = t * UPT + u
                    look = not (last and u == UPT - 1)
                    for q in range(STEPS):
                        j, c = q // SPT, q % SPT
                        step = u * STEPS + q
                        if u == UPT - 1 and not last and q == AT_PERMUTE:
                            act.wait_ge(gathered, t * (16 * FIELDS) + 2 * 16 * FIELDS)
                            act.wait_ge(macs, unit * (STEPS // 2 * HB) + MAC0)
                            act.wait_ge(scaled_done, unit * (STEPS // 2) + SCALED0)
                            permute(0, UPT - 1)
                        if u == 0 and q == AT_PERMUTE:
                            act.wait_ge(macs, unit * (STEPS // 2 * HB) + MAC0)
                            act.wait_ge(scaled_done, unit * (STEPS // 2) + SCALED0)
                            permute(UPT - 1, UPT)
                        if look and q == AT_EVACUATE:
                            evacuate(unit + 1)
                        if look and q == AT_HI5:
                            hi5(unit + 1)
                        if look and q == AT_HI:
                            hi(unit + 1, (u + 1) % 2)
                        if q % 2 == 0:
                            continue
                        if c == 1:
                            act.wait_ge(sums_done, unit * J + (j + 1))
                        act.wait_ge(y_ready, t * (UPT * STEPS) + (step + 1))
                        for r in range(HB):
                            h = c * HB + r
                            last_mul = nc.scalar.mul(scaled[:, (u % 2) * J + j, c // 2 * HB + r, :],
                                                     y_ps[step % YB][:, r, :], x[:, u, j, h:h + 1])
                        last_mul.then_inc(scaled_done, 1)

            batch_tiles(act, body)

            act.wait_ge(z2t_ready, 1)
            nc.scalar.copy(z2_t[:, :], xt_ps[:, :]).then_inc(z2t_copied, 1)
            for m in range(MLP1 // P):
                act.wait_ge(h1_ready, m + 1)
                nc.scalar.activation(h1[:, m * BATCH:(m + 1) * BATCH], y_ps[m][:, :, :].rearrange("p h n -> p (h n)"),
                                     ACT.Relu, bias=bt1_sb[:, m:m + 1]).then_inc(h1_done, 1)
            for m in range(MLP2 // P):
                act.wait_ge(h2_ready, 1)
                nc.scalar.activation(h2[:, m * BATCH:(m + 1) * BATCH], y_ps[4 + m][:, :, :].rearrange("p h n -> p (h n)"),
                                     ACT.Relu, bias=bt2_sb[:, m:m + 1]).then_inc(h2_done, 1)
            act.wait_ge(row_ready, 1)
            nc.scalar.copy(y_row[:, :], cur_ps[0:1, :]).then_inc(row_copied, 1)

        @block.vector
        def _(dve):
            def product(unit, c):
                if c == 0:
                    dve.wait_ge(ab_loaded, unit * (16 * LOADS) + 16 * LOADS)
                out_, b_ = (z[:, c, :], b_rows[:, c, :]) if c < CHUNKS else (zs[:, :], bs_rows[:, :])
                nc.vector.tensor_tensor(out_, a_rows[:, :], b_, ALU.mult).then_inc(products, 1)

            def lo5(unit):
                half = slice(P // 2, P)
                dve.wait_ge(hi5_done, unit + 1)
                nc.vector.tensor_tensor(zp[half, :], zs[half, :], zp[half, :].bitcast(f32),
                                        ALU.subtract).then_inc(lo5_done, 1)

            def lo(unit, parity):
                dve.wait_ge(hi_done, unit + 1)
                nc.vector.scalar_tensor_tensor(cur_lo[:, parity, :], cur_ps[:, :], 0.0,
                                               cur_hi[:, parity, :].bitcast(f32), ALU.max,
                                               ALU.subtract).then_inc(lo_done, 1)

            def add_z1(unit, u, t):
                flat = z1[:, :, :].rearrange("p j b -> p (j b)")
                if u == 0:
                    nc.vector.tensor_scalar(flat, cur_ps[:, :], 0.0, None, ALU.max).then_inc(z1_added, 1)
                else:
                    dve.wait_ge(z1_added, unit)
                    nc.vector.scalar_tensor_tensor(flat, cur_ps[:, :], 0.0, flat, ALU.max, ALU.add).then_inc(z1_added, 1)
                if u == UPT - 1:
                    dve.wait_ge(z1_added, unit + 1)
                    nc.vector.tensor_reduce(z1_all[:, bass.ts(t, P)], z1[:, :, :].rearrange("p j b -> p b j"),
                                            AX.X, ALU.add).then_inc(z1_reduced, 1)

            def finish(unit, parity, u, part):
                if part == 0:
                    dve.wait_ge(macs, (unit + 1) * (STEPS // 2 * HB) + MAC0)
                    nc.vector.tensor_tensor(total[:, :, :], acc[:, parity, 0, :, :], acc[:, parity, 1, :, :],
                                            ALU.add).then_inc(finish_chain, 1)
                elif part == 1:
                    dve.wait_ge(sums_done, (unit + 1) * J + SUMS0)
                    dve.wait_ge(finish_chain, (unit + 1) * 2 + 1)
                    nc.vector.tensor_tensor(total[:, :, :], total[:, :, :], sums[:, parity, :, :],
                                            ALU.add).then_inc(finish_chain, 1)
                elif part == 2:
                    dve.wait_ge(finish_chain, (unit + 1) * 2 + 2)
                    if u == 0:
                        nc.vector.tensor_scalar(z2[:, :, :], total[:, :, :], 0.0, None, ALU.max).then_inc(finished, 1)
                    else:
                        dve.wait_ge(finished, (unit + 1) + FINISHED0)
                        nc.vector.scalar_tensor_tensor(z2[:, :, :], total[:, :, :], 0.0, z2[:, :, :],
                                                       ALU.max, ALU.add).then_inc(finished, 1)

            def reduce_z2(unit, slot):
                dve.wait_ge(finished, (unit + 1) + (FINISHED0 + 1))
                nc.vector.tensor_reduce(z2_all[:, slot, :], z2[:, :, :].rearrange("p j n -> p n j"),
                                        AX.X, ALU.add).then_inc(z2_reduced, 1)

            nc.vector.memset(acc[:, 1, :, :, :], 0.0).then_inc(macs, MAC0)
            nc.vector.memset(z2[:, :, :], 0.0).then_inc(finished, FINISHED0)
            dve.wait_ge(f0_in, 48)
            nc.vector.tensor_tensor(f0[:, :, :], fa[:, :, :], fb[:, :, :], ALU.add).then_inc(f0_folded, 1)
            nc.vector.tensor_copy(f0p[:, :], f0s[:, :]).then_inc(f0_parted, 1)
            dve.wait_ge(f0_folded, 1)
            nc.vector.tensor_copy(f0[0:FIELDS, 0, :], fa[0:FIELDS, 0, :]).then_inc(f0_folded, 1)
            dve.wait_ge(f0_parted, 1)
            for g in (1, 3):
                part = slice(g * FIELDS, (g + 1) * FIELDS)
                nc.vector.tensor_tensor(f0p[part, :], f0s[part, :], f0p[part, :].bitcast(f32),
                                        ALU.subtract).then_inc(f0_parted, 1)
            dve.wait_ge(f1_hi_done, 1)
            nc.vector.tensor_tensor(f1_lo[:, :], f1_raw, f1_hi[:, :].bitcast(f32), ALU.subtract).then_inc(f1_split, 1)
            for c in range(CHUNKS + 1):
                product(0, c)
            lo5(0)
            lo(0, 0)
            add_z1(0, 0, 0)

            def body(t, last):
                for u in range(UPT):
                    unit = t * UPT + u
                    look = not (last and u == UPT - 1)
                    for q in range(STEPS):
                        j, c = q // SPT, q % SPT
                        step = u * STEPS + q
                        if AT_FINISH <= q < AT_FINISH + 3:
                            finish(unit - 1, (u + 1) % 2, (u - 1) % UPT, q - AT_FINISH)
                        if u == 0 and q == AT_FINISH + 3:
                            reduce_z2(unit - 1, t)
                        if look and AT_PRODUCTS <= q <= AT_PRODUCTS + CHUNKS:
                            product(unit + 1, q - AT_PRODUCTS)
                        if look and q == AT_LO5 + 1:
                            lo5(unit + 1)
                        if look and q == AT_LO:
                            lo(unit + 1, (u + 1) % 2)
                        if look and q == AT_LO + 1:
                            add_z1(unit + 1, (u + 1) % UPT, t)
                        if q == 0:
                            dve.wait_ge(finished, unit + 1)
                        if q % 2 == 1:
                            continue
                        dve.wait_ge(y_ready, t * (UPT * STEPS) + (step + 1))
                        for r in range(HB):
                            h = c * HB + r
                            y, a, scalar = y_ps[step % YB][:, r, :], acc[:, u % 2, r % SUMS, j, :], x[:, u, j, h:h + 1]
                            if c == 0 and r < SUMS:
                                nc.vector.tensor_scalar(a, y, scalar, None, ALU.mult).then_inc(macs, 1)
                            else:
                                n = step // 2 * HB + r
                                dve.wait_ge(macs, t * (UPT * STEPS // 2 * HB) + (MAC0 + n - SUMS + 1))
                                nc.vector.scalar_tensor_tensor(a, y, scalar, a, ALU.mult, ALU.add).then_inc(macs, 1)

            batch_tiles(dve, body)
            for part in range(3):
                finish(UNITS - 1, (UNITS - 1) % 2, UPT - 1, part)
            reduce_z2(UNITS - 1, BT)


def kernel(**inputs):
    import numpy as _np
    import concourse.bacc as _bacc
    from concourse import mybir as _mybir
    from concourse.bass_utils import run_bass_kernel_spmd as _run

    nc = _bacc.Bacc("TRN2", target_bir_lowering=False, num_devices=1)
    arrays = {}

    def put(name, a):
        a = _np.ascontiguousarray(a)
        arrays[name] = a
        return nc.dram_tensor(name, a.shape, _mybir.dt.from_np(a.dtype), kind="ExternalInput").ap()

    i = _np.arange(FIELDS)
    s = REP * _np.arange(CHUNKS)[None, :, None] + _np.arange(REP)[:, None, None]
    k = (i[None, None, :] + s) % FIELDS
    pair_a = (i * FIELDS + k).transpose(0, 2, 1).reshape(P, CHUNKS)
    pair_b = (k * FIELDS + i).transpose(0, 2, 1).reshape(P, CHUNKS)
    pair_s = _np.tile(i * FIELDS + (i + FIELDS // 2) % FIELDS, REP)
    filter_0 = _np.asarray(inputs["L0_rec_filter_0"])[0]
    args = [
        put("ids", inputs["ids"]),
        [put(f"tbl_{h}", inputs[f"tbl_{h}"]) for h in range(FIELDS)],
        put("w1a", filter_0[pair_a]),
        put("w1b", filter_0[pair_b]),
        put("w1s", filter_0[pair_s]),
        put("f1", _np.asarray(inputs["L0_rec_filter_1"])[0]),
        put("eye", _np.eye(P, dtype=_np.float32)),
        put("dense_t", _np.asarray(inputs["dense_ctx"]).T),
        put("wt1", inputs["W_top1"]),
        put("bt1", _np.asarray(inputs["b_top1"]).reshape(MLP1 // P, P).T),
        put("wt2", inputs["W_top2"]),
        put("bt2", _np.asarray(inputs["b_top2"]).reshape(MLP2 // P, P).T),
        put("wt3", _np.asarray(inputs["W_top3"]).reshape(MLP2 // P, P).T),
    ]
    out = nc.dram_tensor("out", (BATCH, 1), _mybir.dt.float32, kind="ExternalOutput").ap()
    tower(nc, *args, out)
    r = _run(nc, [arrays], core_ids=[0])
    return r.results[0]["out"]
```

```python
import numpy as np
import concourse.bass as bass
from concourse import mybir
from contextlib import ExitStack

P = 128
BATCH, FIELDS, COLS, FEATS = 512, 32, 32, 128
BT = BATCH // P
J = 4
UPT = COLS // J
UNITS = BT * UPT
W = J * P
REP = P // FIELDS
CHUNKS = (FIELDS // 2) // REP
HB = 4
SPT = FIELDS // HB
STEPS = J * SPT
SUMS = 2
YB = 6
TR = 2 * J
OWNERS = ["SVSVSVSV", "SVSSVSSV"]
OWNER = "".join(OWNERS[j // 2] for j in range(J))
ROWS = max(o.count("S") for o in OWNERS) * HB
MLP1, MLP2, DENSE = 512, 256, 16
MLP_TILES = [(0, BT - 1), (BT - 1, BT)]

AT_PERMUTE, AT_TRANSPOSE, AT_EVACUATE = 1, 5, 7
AT_PRODUCT = [2, 4, 7, 8, 12]
AT_LAYER1 = [7, 10, 11, 16, 18]
AT_HI5, AT_LO5, AT_HI, AT_LO, AT_Z1 = 13, 15, 17, 23, 27
AT_FINISH = [23, 26, 28]
EARLY = UPT - 2
GATHERS = [8, 6, 6, 6, 6, 0, 0, 0]

MAC0, SCALED0, SUMS0, FINISHED0 = YB * HB, YB * SUMS, TR, 1
LOADS = REP + 2


def steps_of(who, q):
    if q < 0:
        return -sum(OWNER[i % STEPS] == who for i in range(q + 1, 0))
    return sum(OWNER[i % STEPS] == who for i in range(q + 1))


MACS_PU = HB * steps_of("V", STEPS - 1)
SCALED_PU = SUMS * steps_of("S", STEPS - 1)


def tree(n):
    sizes = []
    while n > 2:
        sizes.append((n, n // 2))
        n -= n // 2
    return sizes


TREES = [tree(o.count("S") * HB - SUMS) for o in OWNERS]
LEVELS_PU = sum(len(x) for x in TREES)


def bank_before(q):
    n = UPT * STEPS
    return q - YB if q >= YB else max(x for x in range(n - YB, n) if x % YB == q) - n


def tower(nc, ids, tables, w1a, w1b, w1s, f1, eye, dense_t, wt1, bt1, wt2, bt2, wt3, out):
    f32, f32r, i32 = mybir.dt.float32, mybir.dt.float32r, mybir.dt.int32
    ALU, ACT, AX = mybir.AluOpType, mybir.ActivationFunctionType, mybir.AxisListType
    ctx = ExitStack()
    with ctx:
        def sb(name, shape, dt=f32):
            return ctx.enter_context(nc.sbuf_tensor(name, shape, dt))

        def sem(name):
            return ctx.enter_context(nc.semaphore(name))

        ids_all = sb("ids_all", [P, BT, FIELDS], i32)
        ids_next = sb("ids_next", [P, FIELDS], i32)
        rows = sb("rows", [P, FIELDS, COLS])
        x = sb("x", [P, UPT, J, FIELDS])
        ident = sb("ident", [P, P])
        xt = sb("xt", [P, P])
        xt_dram = nc.dram_tensor("xt_dram", (2 * FIELDS, J, P), f32, kind="Internal").ap()
        fa = sb("fa", [P, CHUNKS, FEATS])
        fb = sb("fb", [P, CHUNKS, FEATS])
        f0 = sb("f0", [P, CHUNKS, FEATS])
        f0s = sb("f0s", [P, FEATS])
        f0p = sb("f0p", [P, FEATS], f32r)
        a_rows = sb("a_rows", [P, W])
        b_rows = sb("b_rows", [P, CHUNKS, W])
        bs_rows = sb("bs_rows", [P, W])
        z = sb("z", [P, CHUNKS, W])
        zs = sb("zs", [P, W])
        zp = sb("zp", [P, W], f32r)
        f1_hi = sb("f1_hi", [P, FIELDS * FEATS], f32r)
        f1_lo = sb("f1_lo", [P, FIELDS * FEATS], f32r)
        cur_hi = sb("cur_hi", [P, 2, W], f32r)
        cur_lo = sb("cur_lo", [P, 2, W], f32r)
        acc = sb("acc", [P, 2, SUMS, J, FEATS])
        scaled = sb("scaled", [P, TR, ROWS, FEATS])
        sums = sb("sums", [P, 2, J, FEATS])
        total = sb("total", [P, J, FEATS])
        scratch = scaled[:, :, :, :].rearrange("p t r n -> p (t r n)")
        f1_raw = scratch[:, 0:FIELDS * FEATS]
        z1 = sb("z1", [P, J, P])
        z2 = sb("z2", [P, J, FEATS])
        z1_all = sb("z1_all", [P, BT * P])
        z2_all = sb("z2_all", [P, BT + 1, FEATS])
        z2_t = sb("z2_t", [P, BATCH])
        dense_sb = sb("dense_sb", [DENSE, BATCH])
        wt1_sb = sb("wt1_sb", [P, 2, MLP1])
        wt1_d = sb("wt1_d", [DENSE, MLP1])
        wt2_sb = sb("wt2_sb", [P, MLP1 // P, MLP2])
        wt3_sb = sb("wt3_sb", [P, MLP2 // P])
        bt1_sb = sb("bt1_sb", [P, MLP1 // P])
        bt2_sb = sb("bt2_sb", [P, MLP2 // P])
        h1_size, h2_size = MLP1 // P * BATCH, MLP2 // P * BATCH
        h1 = scratch[:, 0:h1_size].rearrange("p (k b) -> p k b", b=BATCH)
        h2 = scratch[:, h1_size:h1_size + h2_size].rearrange("p (k b) -> p k b", b=BATCH)
        y_row = sb("y_row", [1, BATCH])

        y_ps = [ctx.enter_context(nc.psum_tensor(f"y_ps{i}", [P, HB, FEATS], f32)) for i in range(YB)]
        cur_ps = ctx.enter_context(nc.psum_tensor("cur_ps", [P, W], f32))
        xt_ps = ctx.enter_context(nc.psum_tensor("xt_ps", [P, W], f32))

        def mlp_ps(g, bank, shared_bank, m):
            lo_t, hi_t = MLP_TILES[g]
            flat = y_ps[bank + m if g == 0 else shared_bank][:, :, :].rearrange("p h n -> p (h n)")
            return flat[:, 0:(hi_t - lo_t) * P] if g == 0 else flat[:, m * P:(m + 1) * P]

        def h1_ps(g, m):
            return mlp_ps(g, 0, 0, m)

        def h2_ps(g, m):
            return mlp_ps(g, MLP1 // P, 1, m)


        ids_in = sem("ids_in")
        eye_in = sem("eye_in")
        f0_in = sem("f0_in")
        f1_in = sem("f1_in")
        mlp_in = sem("mlp_in")
        f0_folded = sem("f0_folded")
        f0_parted = sem("f0_parted")
        f1_hi_done = sem("f1_hi_done")
        f1_split = sem("f1_split")
        ids_staged = sem("ids_staged")
        gathered = sem("gathered")
        permuted = sem("permuted")
        transposed = sem("transposed")
        xt_ready = sem("xt_ready")
        xt_stored = sem("xt_stored")
        ab_loaded = sem("ab_loaded")
        products = sem("products")
        hi5_done = sem("hi5_done")
        lo5_done = sem("lo5_done")
        cur_done = sem("cur_done")
        hi_done = sem("hi_done")
        lo_done = sem("lo_done")
        z1_added = sem("z1_added")
        z1_reduced = sem("z1_reduced")
        y_ready = sem("y_ready")
        macs = sem("macs")
        scaled_done = sem("scaled_done")
        pool_chain = sem("pool_chain")
        sums_done = sem("sums_done")
        finish_chain = sem("finish_chain")
        finished = sem("finished")
        z2_reduced = sem("z2_reduced")
        cleared = sem("cleared")
        z2t_ready = sem("z2t_ready")
        z2t_copied = sem("z2t_copied")
        h1_ready = sem("h1_ready")
        h1_done = sem("h1_done")
        h2_ready = sem("h2_ready")
        h2_done = sem("h2_done")
        row_ready = sem("row_ready")
        row_copied = sem("row_copied")
        out_stored = sem("out_stored")

        block = ctx.enter_context(nc.Block())

        def batch_tiles(engine, body):
            with engine.Fori(0, BT - 1) as t:
                body(t, False)
            body(BT - 1, True)

        @block.sync
        def _(sp):
            sp.dma_start(ids_all[:, :, :], ids.rearrange("(t p) f -> p t f", p=P)).then_inc(ids_in, 16)
            sp.dma_start(ident[:, :], eye).then_inc(eye_in, 16)
            sp.dma_start(fa[:, :, :], w1a).then_inc(f0_in, 16)
            sp.dma_start(fb[:, :, :], w1b).then_inc(f0_in, 16)
            sp.dma_start(f0s[:, :], w1s).then_inc(f0_in, 16)
            sp.dma_start(f1_raw.rearrange("m (h n) -> m h n", n=FEATS),
                         f1.rearrange("(h m) n -> m h n", m=FEATS)).then_inc(f1_in, 16)
            sp.dma_start(wt1_sb[:, :, :], wt1[0:2 * P, :].rearrange("(k p) n -> p k n", p=P)).then_inc(mlp_in, 16)
            sp.dma_start(wt1_d[:, :], wt1[2 * P:2 * P + DENSE, :]).then_inc(mlp_in, 16)
            sp.dma_start(wt2_sb[:, :, :], wt2.rearrange("(k p) n -> p k n", p=P)).then_inc(mlp_in, 16)
            sp.dma_start(wt3_sb[:, :], wt3).then_inc(mlp_in, 16)
            sp.dma_start(bt1_sb[:, :], bt1).then_inc(mlp_in, 16)
            sp.dma_start(bt2_sb[:, :], bt2).then_inc(mlp_in, 16)
            sp.dma_start(dense_sb[:, :], dense_t).then_inc(mlp_in, 16)

            def spread(unit):
                first = isinstance(unit, int)
                here, stored, read, made = [v if first else sp.to_reg(v) for v in (
                    unit + 1, unit * 32 + 32, unit * (16 * LOADS), unit * (CHUNKS + 1))]
                if not first:
                    sp.wait_ge(ab_loaded, read)
                sp.wait_ge(xt_ready, here)
                for half in range(2):
                    dst = xt_dram[half * FIELDS:(half + 1) * FIELDS, :, :]
                    sp.dma_start(bass.AP(dst.tensor, dst.offset, [[P, J], [W, FIELDS], [1, P]]),
                                 xt[:, :]).then_inc(xt_stored, 16)
                if not first:
                    sp.wait_ge(products, made)
                sp.wait_ge(xt_stored, stored)
                for r in range(REP):
                    part = slice(r * FIELDS, (r + 1) * FIELDS)
                    src = xt_dram[r:r + FIELDS, :, :]
                    rotated = bass.AP(src.tensor, src.offset, [[W, FIELDS], [REP * W, CHUNKS], [1, W]])
                    sp.dma_start(b_rows[part, :, :], rotated).then_inc(ab_loaded, 16)
                for dst, at in ((a_rows, 0), (bs_rows, FIELDS // 2)):
                    src = xt_dram[at:at + FIELDS, :, :]
                    repeated = bass.AP(src.tensor, src.offset, [[0, REP], [W, FIELDS], [1, W]])
                    sp.dma_start(dst[:, :], repeated).then_inc(ab_loaded, 16)

            spread(0)
            with sp.Fori(1, UNITS) as unit:
                spread(unit)
            sp.wait_ge(row_copied, 1)
            sp.dma_start(out.rearrange("b o -> o b"), y_row[:, :]).then_inc(out_stored, 16)
            sp.wait_ge(out_stored, 16)

        @block.gpsimd
        def _(pool):
            def gather(h, ids_tile):
                pool.indirect_dma_start(
                    out=rows[:, h, :], out_offset=None, in_=tables[h],
                    in_offset=bass.IndirectOffsetOnAxis(ap=ids_tile[:, h:h + 1], axis=0)).then_inc(gathered, 16)

            pool.wait_ge(ids_in, 16)
            for h in range(FIELDS):
                gather(h, ids_all[:, 0, :])
            nc.gpsimd.memset(sums[:, 1, :, :], 0.0).then_inc(sums_done, SUMS0)

            def add_up(unit, u, pair, staged=None):
                if staged is not None:
                    pool.wait_ge(ids_staged, staged)
                last_step = (u * J + 2 * pair + 2) * SPT - 1
                pool.wait_ge(scaled_done, (unit - u) * SCALED_PU + (SCALED0 + SUMS * steps_of("S", last_step)))
                first = (u % 2) * J + 2 * pair
                t = scaled[:, first:first + 2, SUMS:ROWS, :]
                level = sum(len(x) for x in TREES[:pair])
                for n, half in TREES[pair]:
                    nc.gpsimd.tensor_tensor(t[:, :, 0:half, :], t[:, :, 0:half, :], t[:, :, n - half:n, :],
                                            ALU.add).then_inc(pool_chain, 1)
                    level += 1
                    pool.wait_ge(pool_chain, unit * LEVELS_PU + level)
                if pair == 0:
                    pool.wait_ge(finished, unit + 1)
                nc.gpsimd.tensor_tensor(sums[:, u % 2, 2 * pair:2 * pair + 2, :], t[:, :, 0, :], t[:, :, 1, :],
                                        ALU.add).then_inc(sums_done, 2)

            def body(t, last):
                h = 0
                for u in range(UPT):
                    unit = t * UPT + u
                    if u == 0 and not last:
                        pool.wait_ge(permuted, t * 2 + 2)
                        nc.gpsimd.tensor_copy(ids_next[:, :], ids_all[:, t + 1, :]).then_inc(ids_staged, 1)
                    for pair in range(2):
                        add_up(unit, u, pair, t + 1 if u == 0 and pair == 0 and not last else None)
                        if not last:
                            for _ in range(GATHERS[u] // 2):
                                gather(h, ids_next)
                                h += 1

            batch_tiles(pool, body)

        @block.tensor
        def _(pe):
            def transpose(unit, dg, need):
                pe.wait_ge(permuted, need)
                if not isinstance(unit, int) or unit > 0:
                    pe.wait_ge(xt_ready, unit)
                nc.tensor.transpose(xt_ps[:, 0:P], x[:, dg, :, :], ident[:, :]).then_inc(transposed, 1)

            def layer1(unit, c, first=False):
                if c == 0 and not first:
                    pe.wait_ge(z1_added, unit)
                    pe.wait_ge(lo_done, unit)
                    pe.wait_ge(hi_done, unit)
                if c < CHUNKS:
                    pe.wait_ge(products, unit * (CHUNKS + 1) + (c + 1))
                    nc.tensor.matmul(cur_ps[:, :], f0[:, c, :], z[:, c, :], start=(c == 0), stop=False)
                else:
                    pe.wait_ge(lo5_done, unit + 1)
                    nc.tensor.matmul(cur_ps[:, :], f0p[:, :], zp[:, :], start=False, stop=True).then_inc(cur_done, 1)

            pe.wait_ge(eye_in, 16)
            transpose(0, 0, 1)
            transpose(1, 1, 1)
            pe.wait_ge(f0_folded, 2)
            pe.wait_ge(f0_parted, 3)
            for c in range(CHUNKS + 1):
                layer1(0, c, first=True)
            pe.wait_ge(f1_split, 1)

            def body(t, last):
                for u in range(UPT):
                    unit = t * UPT + u
                    look, look2 = not (last and u == UPT - 1), not (last and u >= UPT - 2)
                    for q in range(STEPS):
                        j, c = q // SPT, q % SPT
                        step = u * STEPS + q
                        if look2 and q == AT_TRANSPOSE:
                            dg = (u + 2) % UPT
                            transpose(unit + 2, dg, t * 2 + (3 if u + 2 >= UPT else 1 if dg < EARLY else 2))
                        if look and q in AT_LAYER1:
                            layer1(unit + 1, AT_LAYER1.index(q))
                        if q == 0:
                            pe.wait_ge(hi_done, unit + 1)
                            pe.wait_ge(lo_done, unit + 1)
                        before = bank_before(step)
                        if OWNER[before % STEPS] == "V":
                            pe.wait_ge(macs, t * (UPT * MACS_PU) + (MAC0 + HB * steps_of("V", before)))
                        else:
                            pe.wait_ge(scaled_done, t * (UPT * SCALED_PU) + (SCALED0 + SUMS * steps_of("S", before)))
                        bank = y_ps[step % YB][:, :, :].rearrange("p h n -> p (h n)")
                        cols = slice(c * W, (c + 1) * W)
                        hi = cur_hi[:, u % 2, j * P:(j + 1) * P]
                        lo = cur_lo[:, u % 2, j * P:(j + 1) * P]
                        nc.tensor.matmul(bank, hi, f1_hi[:, cols], start=True, stop=False)
                        nc.tensor.matmul(bank, hi, f1_lo[:, cols], start=False, stop=False)
                        nc.tensor.matmul(bank, lo, f1_hi[:, cols], start=False, stop=True).then_inc(y_ready, 1)

            batch_tiles(pe, body)

            pe.wait_ge(mlp_in, 16 * 7)
            pe.wait_ge(macs, MAC0 + UNITS * MACS_PU)
            pe.wait_ge(scaled_done, SCALED0 + UNITS * SCALED_PU)
            pe.wait_ge(z1_reduced, BT)
            pe.wait_ge(xt_ready, UNITS)
            for g, (lo_t, hi_t) in enumerate(MLP_TILES):
                b = slice(lo_t * P, hi_t * P)
                if g == 1:
                    pe.wait_ge(z2t_copied, 1)
                    pe.wait_ge(h1_done, MLP1 // P)
                    pe.wait_ge(h2_done, MLP2 // P)
                pe.wait_ge(z2_reduced, hi_t + 1)
                for t in range(lo_t, hi_t):
                    last = nc.tensor.transpose(xt_ps[:, t * P:(t + 1) * P], z2_all[:, t + 1, :], ident[:, :])
                last.then_inc(z2t_ready, 1)
                for m in range(MLP1 // P):
                    cols = slice(m * P, (m + 1) * P)
                    if g == 0:
                        nc.tensor.matmul(h1_ps(g, m), wt1_sb[:, 0, cols], z1_all[:, b], start=True, stop=False)
                        nc.tensor.matmul(h1_ps(g, m), wt1_d[:, cols], dense_sb[:, b], start=False, stop=False)
                for m in range(MLP1 // P):
                    cols = slice(m * P, (m + 1) * P)
                    if g == 1:
                        nc.tensor.matmul(h1_ps(g, m), wt1_sb[:, 0, cols], z1_all[:, b], start=True, stop=False)
                        nc.tensor.matmul(h1_ps(g, m), wt1_d[:, cols], dense_sb[:, b], start=False, stop=False)
                    if m == 0:
                        pe.wait_ge(z2t_copied, g + 1)
                    nc.tensor.matmul(h1_ps(g, m), wt1_sb[:, 1, cols], z2_t[:, b], start=False,
                                     stop=True).then_inc(h1_ready, 1)
                for m in range(MLP2 // P):
                    for k in range(MLP1 // P):
                        pe.wait_ge(h1_done, g * (MLP1 // P) + k + 1)
                        last = nc.tensor.matmul(h2_ps(g, m), wt2_sb[:, k, m * P:(m + 1) * P], h1[:, k, b],
                                                start=(k == 0), stop=(k == MLP1 // P - 1))
                    last.then_inc(h2_ready, 1)
                for k in range(MLP2 // P):
                    pe.wait_ge(h2_done, g * (MLP2 // P) + k + 1)
                    last = nc.tensor.matmul(cur_ps[0:1, b], wt3_sb[:, k:k + 1], h2[:, k, b],
                                            start=(k == 0), stop=(k == MLP2 // P - 1))
                last.then_inc(row_ready, 1)

        @block.scalar
        def _(act):
            def evacuate(unit, first=False):
                act.wait_ge(transposed, unit + 1)
                if not first:
                    act.wait_ge(xt_stored, unit * 32)
                nc.scalar.copy(xt[:, :], xt_ps[:, 0:P]).then_inc(xt_ready, 1)

            def hi5(unit):
                act.wait_ge(products, unit * (CHUNKS + 1) + (CHUNKS + 1))
                nc.scalar.copy(zp[:, :], zs[:, :]).then_inc(hi5_done, 1)

            def hi(unit, parity):
                act.wait_ge(cur_done, unit + 1)
                nc.scalar.activation(cur_hi[:, parity, :], cur_ps[:, :], ACT.Relu).then_inc(hi_done, 1)

            def permute(a, b):
                nc.scalar.copy(x[:, a:b, :, :].rearrange("p g j h -> p (g j) h"),
                               rows[:, :, a * J:b * J].rearrange("p h d -> p d h")).then_inc(permuted, 1)

            act.preload_act_table(ACT.Relu)
            act.sem_inc(scaled_done, SCALED0)
            act.wait_ge(f1_in, 16)
            nc.scalar.copy(f1_hi[:, :], f1_raw).then_inc(f1_hi_done, 1)
            act.wait_ge(gathered, 16 * FIELDS)
            permute(0, EARLY)
            evacuate(0, first=True)
            evacuate(1)
            hi5(0)
            hi(0, 0)

            def body(t, last):
                for u in range(UPT):
                    unit = t * UPT + u
                    look, look2 = not (last and u == UPT - 1), not (last and u >= UPT - 2)
                    for q in range(STEPS):
                        j, c = q // SPT, q % SPT
                        step = u * STEPS + q
                        if u == EARLY and not last and q == AT_PERMUTE:
                            act.wait_ge(gathered, t * (16 * FIELDS) + 2 * 16 * FIELDS)
                            act.wait_ge(macs, unit * MACS_PU + MAC0)
                            act.wait_ge(scaled_done, unit * SCALED_PU + SCALED0)
                            permute(0, EARLY)
                        if u == 0 and q == AT_PERMUTE:
                            act.wait_ge(macs, unit * MACS_PU + MAC0)
                            act.wait_ge(scaled_done, unit * SCALED_PU + SCALED0)
                            permute(EARLY, UPT)
                        if look2 and q == AT_EVACUATE:
                            evacuate(unit + 2)
                        if look and q == AT_HI5:
                            hi5(unit + 1)
                        if look and q == AT_HI:
                            hi(unit + 1, (u + 1) % 2)
                        if OWNER[q] != "S":
                            continue
                        if c == 0:
                            act.wait_ge(sums_done, unit * J + (j + 1))
                        act.wait_ge(y_ready, t * (UPT * STEPS) + (step + 1))
                        row = HB * OWNER[j * SPT:q].count("S")
                        for r in range(HB):
                            h = c * HB + r
                            mul = nc.scalar.mul(scaled[:, (u % 2) * J + j, row + r, :],
                                                y_ps[step % YB][:, r, :], x[:, u, j, h:h + 1])
                            if (r + 1) % (HB // SUMS) == 0:
                                mul.then_inc(scaled_done, 1)

            batch_tiles(act, body)

            for g, (lo_t, hi_t) in enumerate(MLP_TILES):
                b = slice(lo_t * P, hi_t * P)
                act.wait_ge(z2t_ready, g + 1)
                nc.scalar.copy(z2_t[:, b], xt_ps[:, b]).then_inc(z2t_copied, 1)
                for m in range(MLP1 // P):
                    act.wait_ge(h1_ready, g * (MLP1 // P) + m + 1 if g == 0 else (g + 1) * (MLP1 // P))
                    nc.scalar.activation(h1[:, m, b], h1_ps(g, m), ACT.Relu,
                                         bias=bt1_sb[:, m:m + 1]).then_inc(h1_done, 1)
                for m in range(MLP2 // P):
                    act.wait_ge(h2_ready, g * (MLP2 // P) + m + 1 if g == 0 else (g + 1) * (MLP2 // P))
                    nc.scalar.activation(h2[:, m, b], h2_ps(g, m), ACT.Relu,
                                         bias=bt2_sb[:, m:m + 1]).then_inc(h2_done, 1)
            act.wait_ge(row_ready, 2)
            nc.scalar.copy(y_row[:, :], cur_ps[0:1, :]).then_inc(row_copied, 1)

        @block.vector
        def _(dve):
            def product(unit, c):
                if c == 0:
                    dve.wait_ge(ab_loaded, unit * (16 * LOADS) + 16 * LOADS)
                out_, b_ = (z[:, c, :], b_rows[:, c, :]) if c < CHUNKS else (zs[:, :], bs_rows[:, :])
                nc.vector.tensor_tensor(out_, a_rows[:, :], b_, ALU.mult).then_inc(products, 1)

            def lo5(unit):
                half = slice(P // 2, P)
                dve.wait_ge(hi5_done, unit + 1)
                nc.vector.tensor_tensor(zp[half, :], zs[half, :], zp[half, :].bitcast(f32),
                                        ALU.subtract).then_inc(lo5_done, 1)

            def lo(unit, parity):
                dve.wait_ge(hi_done, unit + 1)
                nc.vector.scalar_tensor_tensor(cur_lo[:, parity, :], cur_ps[:, :], 0.0,
                                               cur_hi[:, parity, :].bitcast(f32), ALU.max,
                                               ALU.subtract).then_inc(lo_done, 1)

            def add_z1(unit, u, t):
                flat = z1[:, :, :].rearrange("p j b -> p (j b)")
                if u == 0:
                    nc.vector.tensor_scalar(flat, cur_ps[:, :], 0.0, None, ALU.max).then_inc(z1_added, 1)
                else:
                    dve.wait_ge(z1_added, unit)
                    nc.vector.scalar_tensor_tensor(flat, cur_ps[:, :], 0.0, flat, ALU.max, ALU.add).then_inc(z1_added, 1)
                if u == UPT - 1:
                    dve.wait_ge(z1_added, unit + 1)
                    nc.vector.tensor_reduce(z1_all[:, bass.ts(t, P)], z1[:, :, :].rearrange("p j b -> p b j"),
                                            AX.X, ALU.add).then_inc(z1_reduced, 1)

            def finish(unit, parity, u, part):
                if part == 0:
                    dve.wait_ge(macs, (unit + 1) * MACS_PU + MAC0)
                    nc.vector.tensor_tensor(total[:, :, :], acc[:, parity, 0, :, :], acc[:, parity, 1, :, :],
                                            ALU.add).then_inc(finish_chain, 1)
                elif part == 1:
                    dve.wait_ge(sums_done, (unit + 1) * J + SUMS0)
                    dve.wait_ge(finish_chain, (unit + 1) * 2 + 1)
                    nc.vector.tensor_tensor(total[:, :, :], total[:, :, :], sums[:, parity, :, :],
                                            ALU.add).then_inc(finish_chain, 1)
                elif part == 2:
                    dve.wait_ge(finish_chain, (unit + 1) * 2 + 2)
                    if u == 0:
                        nc.vector.tensor_scalar(z2[:, :, :], total[:, :, :], 0.0, None, ALU.max).then_inc(finished, 1)
                    else:
                        dve.wait_ge(finished, (unit + 1) + FINISHED0)
                        nc.vector.scalar_tensor_tensor(z2[:, :, :], total[:, :, :], 0.0, z2[:, :, :],
                                                       ALU.max, ALU.add).then_inc(finished, 1)

            def reduce_z2(unit, slot):
                dve.wait_ge(finished, (unit + 1) + (FINISHED0 + 1))
                nc.vector.tensor_reduce(z2_all[:, slot, :], z2[:, :, :].rearrange("p j n -> p n j"),
                                        AX.X, ALU.add).then_inc(z2_reduced, 1)

            nc.vector.memset(acc[:, 1, :, :, :], 0.0).then_inc(macs, MAC0)
            nc.vector.memset(z2[:, :, :], 0.0).then_inc(finished, FINISHED0)
            dve.wait_ge(f0_in, 48)
            nc.vector.tensor_tensor(f0[:, :, :], fa[:, :, :], fb[:, :, :], ALU.add).then_inc(f0_folded, 1)
            nc.vector.tensor_copy(f0p[:, :], f0s[:, :]).then_inc(f0_parted, 1)
            dve.wait_ge(f0_folded, 1)
            nc.vector.tensor_copy(f0[0:FIELDS, 0, :], fa[0:FIELDS, 0, :]).then_inc(f0_folded, 1)
            dve.wait_ge(f0_parted, 1)
            for g in (1, 3):
                part = slice(g * FIELDS, (g + 1) * FIELDS)
                nc.vector.tensor_tensor(f0p[part, :], f0s[part, :], f0p[part, :].bitcast(f32),
                                        ALU.subtract).then_inc(f0_parted, 1)
            dve.wait_ge(f1_hi_done, 1)
            nc.vector.tensor_tensor(f1_lo[:, :], f1_raw, f1_hi[:, :].bitcast(f32), ALU.subtract).then_inc(f1_split, 1)
            for c in range(CHUNKS + 1):
                product(0, c)
            lo5(0)
            lo(0, 0)
            add_z1(0, 0, 0)

            def body(t, last):
                for u in range(UPT):
                    unit = t * UPT + u
                    look, look2 = not (last and u == UPT - 1), not (last and u >= UPT - 2)
                    for q in range(STEPS):
                        j, c = q // SPT, q % SPT
                        step = u * STEPS + q
                        if q in AT_FINISH:
                            finish(unit - 1, (u + 1) % 2, (u - 1) % UPT, AT_FINISH.index(q))
                        if u == 0 and q == AT_FINISH[-1]:
                            reduce_z2(unit - 1, t)
                        if look and q in AT_PRODUCT:
                            product(unit + 1, AT_PRODUCT.index(q))
                        if look and q == AT_LO5:
                            lo5(unit + 1)
                        if look and q == AT_LO:
                            lo(unit + 1, (u + 1) % 2)
                        if look and q == AT_Z1:
                            add_z1(unit + 1, (u + 1) % UPT, t)
                        if q == 0:
                            dve.wait_ge(finished, unit + 1)
                        if OWNER[q] != "V":
                            continue
                        start = "V" not in OWNER[j * SPT:q]
                        if start:
                            dve.wait_ge(scaled_done, t * (UPT * SCALED_PU)
                                        + (SCALED0 + SUMS * steps_of("S", u * STEPS + j * SPT - 1) + 1))
                        dve.wait_ge(y_ready, t * (UPT * STEPS) + (step + 1))
                        for r in range(HB):
                            h = c * HB + r
                            a = acc[:, u % 2, r % SUMS, j, :]
                            begun = scaled[:, (u % 2) * J + j, r, :] if start and r < SUMS else a
                            if not (start and r < SUMS):
                                dve.wait_ge(macs, t * (UPT * MACS_PU)
                                            + (MAC0 + HB * steps_of("V", step - 1) + r - SUMS + 1))
                            nc.vector.scalar_tensor_tensor(a, y_ps[step % YB][:, r, :], x[:, u, j, h:h + 1], begun,
                                                           ALU.mult, ALU.add).then_inc(macs, 1)

            batch_tiles(dve, body)
            for part in range(3):
                finish(UNITS - 1, (UNITS - 1) % 2, UPT - 1, part)
            reduce_z2(UNITS - 1, BT)


def kernel(**inputs):
    import numpy as _np
    import concourse.bacc as _bacc
    from concourse import mybir as _mybir
    from concourse.bass_utils import run_bass_kernel_spmd as _run

    nc = _bacc.Bacc("TRN2", target_bir_lowering=False, num_devices=1)
    arrays = {}

    def put(name, a):
        a = _np.ascontiguousarray(a)
        arrays[name] = a
        return nc.dram_tensor(name, a.shape, _mybir.dt.from_np(a.dtype), kind="ExternalInput").ap()

    i = _np.arange(FIELDS)
    s = REP * _np.arange(CHUNKS)[None, :, None] + _np.arange(REP)[:, None, None]
    k = (i[None, None, :] + s) % FIELDS
    pair_a = (i * FIELDS + k).transpose(0, 2, 1).reshape(P, CHUNKS)
    pair_b = (k * FIELDS + i).transpose(0, 2, 1).reshape(P, CHUNKS)
    pair_s = _np.tile(i * FIELDS + (i + FIELDS // 2) % FIELDS, REP)
    filter_0 = _np.asarray(inputs["L0_rec_filter_0"])[0]
    args = [
        put("ids", inputs["ids"]),
        [put(f"tbl_{h}", inputs[f"tbl_{h}"]) for h in range(FIELDS)],
        put("w1a", filter_0[pair_a]),
        put("w1b", filter_0[pair_b]),
        put("w1s", filter_0[pair_s]),
        put("f1", _np.asarray(inputs["L0_rec_filter_1"])[0]),
        put("eye", _np.eye(P, dtype=_np.float32)),
        put("dense_t", _np.asarray(inputs["dense_ctx"]).T),
        put("wt1", inputs["W_top1"]),
        put("bt1", _np.asarray(inputs["b_top1"]).reshape(MLP1 // P, P).T),
        put("wt2", inputs["W_top2"]),
        put("bt2", _np.asarray(inputs["b_top2"]).reshape(MLP2 // P, P).T),
        put("wt3", _np.asarray(inputs["W_top3"]).reshape(MLP2 // P, P).T),
    ]
    out = nc.dram_tensor("out", (BATCH, 1), _mybir.dt.float32, kind="ExternalOutput").ap()
    tower(nc, *args, out)
    r = _run(nc, [arrays], core_ids=[0])
    return r.results[0]["out"]
```

```python
import concourse.bass as bass
from concourse import mybir
from contextlib import ExitStack

P = 128
BATCH, FIELDS, COLS, FEATS = 512, 32, 32, 128
BT = BATCH // P
J = 4
UPT = COLS // J
UNITS = BT * UPT
W = J * P
REP = P // FIELDS
CHUNKS = (FIELDS // 2) // REP
LAST = CHUNKS
PARTS = [(0, 2), (2, CHUNKS), (LAST, LAST + 1)]
LOADS = [3, 2, 1]
SPLIT_PART = 1
SPLIT = slice(*PARTS[SPLIT_PART])
NSPLIT = SPLIT.stop - SPLIT.start
HB = 4
SPT = FIELDS // HB
STEPS = J * SPT
SUMS = 2
YB = 6
TR = 2 * J
OWNERS = ["SVSVSVSV", "SVSVSVSS"]
OWNER = "".join(OWNERS[j // 2] for j in range(J))
ROWS = max(o.count("S") for o in OWNERS) * HB
MLP1, MLP2, DENSE = 512, 256, 16
Z2_PARTS = [(0, BT - 1), (BT - 1, BT)]

AT_PERMUTE, AT_TRANSPOSE, AT_EVACUATE = 1, 5, 7
AT_PRODUCT = [0, 1, 3]
AT_LAYER1 = [5, 11, 12, 16, 19]
AT_Z_HI, AT_Z_LO = 4, 6
AT_HI5, AT_LO5, AT_HI, AT_LO, AT_Z1 = 4, 6, 19, 22, 23
AT_FINISH = [15, 19, 23]
EARLY = UPT - 2
GATHERS = [8, 6, 6, 6, 6, 0, 0, 0]

MAC0, SCALED0, SUMS0, FINISHED0 = YB * HB, YB * SUMS, TR, 1


def steps_of(who, q):
    if q < 0:
        return -sum(OWNER[i % STEPS] == who for i in range(q + 1, 0))
    return sum(OWNER[i % STEPS] == who for i in range(q + 1))


MACS_PU = HB * steps_of("V", STEPS - 1)
SCALED_PU = SUMS * steps_of("S", STEPS - 1)


def tree(n):
    sizes = []
    while n > 2:
        sizes.append((n, n // 2))
        n -= n // 2
    return sizes


TREES = [tree(o.count("S") * HB - SUMS) for o in OWNERS]
LEVELS_PU = sum(len(x) for x in TREES)


def bank_before(q):
    n = UPT * STEPS
    return q - YB if q >= YB else max(x for x in range(n - YB, n) if x % YB == q) - n


def tower(nc, ids, tables, w1a, w1b, w1s, f1, eye, dense_t, wt1, bt1, wt2, bt2, wt3, out):
    f32, f32r, i32 = mybir.dt.float32, mybir.dt.float32r, mybir.dt.int32
    ALU, ACT, AX = mybir.AluOpType, mybir.ActivationFunctionType, mybir.AxisListType
    ctx = ExitStack()
    with ctx:
        def sb(name, shape, dt=f32):
            return ctx.enter_context(nc.sbuf_tensor(name, shape, dt))

        def sem(name):
            return ctx.enter_context(nc.semaphore(name))

        ids_all = sb("ids_all", [P, BT, FIELDS], i32)
        ids_next = sb("ids_next", [P, FIELDS], i32)
        rows = sb("rows", [P, FIELDS, COLS])
        x = sb("x", [P, UPT, J, FIELDS])
        ident = sb("ident", [P, P])
        xt = sb("xt", [P, P])
        xt_dram = nc.dram_tensor("xt_dram", (2 * FIELDS, J, P), f32, kind="Internal").ap()
        f0 = sb("f0", [P, CHUNKS, FEATS])
        f0s = sb("f0s", [P, FEATS])
        f0p = sb("f0p", [P, FEATS], f32r)
        a_rows = sb("a_rows", [P, W])
        b_rows = sb("b_rows", [P, CHUNKS + 1, W])
        z = sb("z", [P, CHUNKS + 1, W])
        f0_hi = sb("f0_hi", [P, NSPLIT, FEATS], f32r)
        f0_lo = sb("f0_lo", [P, NSPLIT, FEATS], f32r)
        z_hi = sb("z_hi", [P, NSPLIT, W], f32r)
        z_lo = sb("z_lo", [P, NSPLIT, W], f32r)
        zp = sb("zp", [P, W], f32r)
        f1_hi = sb("f1_hi", [P, FIELDS * FEATS], f32r)
        f1_lo = sb("f1_lo", [P, FIELDS * FEATS], f32r)
        cur_hi = sb("cur_hi", [P, 2, W], f32r)
        cur_lo = sb("cur_lo", [P, 2, W], f32r)
        acc = sb("acc", [P, 2, SUMS, J, FEATS])
        scaled = sb("scaled", [P, TR, ROWS, FEATS])
        sums = sb("sums", [P, 2, J, FEATS])
        total = sb("total", [P, J, FEATS])
        scratch = scaled[:, :, :, :].rearrange("p t r n -> p (t r n)")
        f1_raw = scratch[:, 0:FIELDS * FEATS]
        fa, fb = [scratch[:, (FIELDS + o * CHUNKS) * FEATS:(FIELDS + (o + 1) * CHUNKS) * FEATS]
                  .rearrange("p (c n) -> p c n", n=FEATS) for o in range(2)]
        raw_end = (FIELDS + 2 * CHUNKS) * FEATS
        dense_raw = scratch[:, raw_end:raw_end + BATCH]
        wt1_d_raw = scratch[:, raw_end + BATCH:raw_end + BATCH + MLP1]
        z1 = sb("z1", [P, J, P])
        z2 = sb("z2", [P, J, FEATS])
        z1_all = sb("z1_all", [P, BT * P])
        z2_all = sb("z2_all", [P, BT + 1, FEATS])
        z2_t = sb("z2_t", [P, BATCH])
        dense_p = sb("dense_p", [P, BATCH], f32r)
        wt1_dp = sb("wt1_dp", [P, MLP1], f32r)
        wt1_sb = sb("wt1_sb", [P, 2, MLP1])
        wt2_sb = sb("wt2_sb", [P, MLP1 // P, MLP2])
        wt3_sb = sb("wt3_sb", [P, MLP2 // P])
        bt1_sb = sb("bt1_sb", [P, MLP1 // P])
        bt2_sb = sb("bt2_sb", [P, MLP2 // P])
        h1_size, h2_size = MLP1 // P * BATCH, MLP2 // P * BATCH
        h1 = scratch[:, 0:h1_size].rearrange("p (k b) -> p k b", b=BATCH)
        h2 = scratch[:, h1_size:h1_size + h2_size].rearrange("p (k b) -> p k b", b=BATCH)
        y_row = scratch[0:1, h1_size + h2_size:h1_size + h2_size + BATCH]

        y_ps = [ctx.enter_context(nc.psum_tensor(f"y_ps{i}", [P, HB, FEATS], f32)) for i in range(YB)]
        cur_ps = ctx.enter_context(nc.psum_tensor("cur_ps", [P, W], f32))
        xt_ps = ctx.enter_context(nc.psum_tensor("xt_ps", [P, W], f32))

        order = [(UPT * STEPS - YB + k) % YB for k in range(YB)]
        h1_ps, h2_ps = [[y_ps[bank][:, :, :].rearrange("p h n -> p (h n)") for bank in banks]
                        for banks in (order[:MLP1 // P], order[MLP1 // P:])]

        ids_in = sem("ids_in")
        eye_in = sem("eye_in")
        f0_in = sem("f0_in")
        f1_in = sem("f1_in")
        mlp_in = sem("mlp_in")
        dense_cleared = sem("dense_cleared")
        dense_in = sem("dense_in")
        dense_parted = sem("dense_parted")
        f0_folded = sem("f0_folded")
        f0_parted = sem("f0_parted")
        f1_hi_done = sem("f1_hi_done")
        f1_split = sem("f1_split")
        ids_staged = sem("ids_staged")
        gathered = sem("gathered")
        permuted = sem("permuted")
        transposed = sem("transposed")
        xt_ready = sem("xt_ready")
        xt_stored = sem("xt_stored")
        ab_loaded = [sem(f"ab{part}_loaded") for part in range(len(PARTS))]
        products = sem("products")
        f0_split = sem("f0_split")
        z_hi_done = sem("z_hi_done")
        z_lo_done = sem("z_lo_done")
        hi5_done = sem("hi5_done")
        lo5_done = sem("lo5_done")
        cur_done = sem("cur_done")
        hi_done = sem("hi_done")
        lo_done = sem("lo_done")
        z1_added = sem("z1_added")
        z1_reduced = sem("z1_reduced")
        y_ready = sem("y_ready")
        macs = sem("macs")
        scaled_done = sem("scaled_done")
        pool_chain = sem("pool_chain")
        sums_done = sem("sums_done")
        last_sum_done = sem("last_sum_done")
        finish_chain = sem("finish_chain")
        finished = sem("finished")
        z2_reduced = sem("z2_reduced")
        cleared = sem("cleared")
        z2t_ready = sem("z2t_ready")
        z2t_copied = sem("z2t_copied")
        h1_ready = sem("h1_ready")
        h1_done = sem("h1_done")
        h2_ready = sem("h2_ready")
        h2_done = sem("h2_done")
        row_ready = sem("row_ready")
        row_copied = sem("row_copied")
        out_stored = sem("out_stored")

        block = ctx.enter_context(nc.Block())

        def batch_tiles(engine, body):
            with engine.Fori(0, BT - 1) as t:
                body(t, False)
            body(BT - 1, True)

        @block.sync
        def _(sp):
            sp.dma_start(ids_all[:, :, :], ids.rearrange("(t p) f -> p t f", p=P)).then_inc(ids_in, 16)
            sp.dma_start(ident[:, :], eye).then_inc(eye_in, 16)
            sp.dma_start(fa[:, :, :], w1a).then_inc(f0_in, 16)
            sp.dma_start(fb[:, :, :], w1b).then_inc(f0_in, 16)
            sp.dma_start(f0s[:, :], w1s).then_inc(f0_in, 16)
            sp.dma_start(f1_raw.rearrange("m (h n) -> m h n", n=FEATS),
                         f1.rearrange("(h m) n -> m h n", m=FEATS)).then_inc(f1_in, 16)
            sp.dma_start(wt1_sb[:, :, :], wt1[0:2 * P, :].rearrange("(k p) n -> p k n", p=P)).then_inc(mlp_in, 16)
            sp.dma_start(wt2_sb[:, :, :], wt2.rearrange("(k p) n -> p k n", p=P)).then_inc(mlp_in, 16)
            sp.dma_start(wt3_sb[:, :], wt3).then_inc(mlp_in, 16)
            sp.dma_start(bt1_sb[:, :], bt1).then_inc(mlp_in, 16)
            sp.dma_start(bt2_sb[:, :], bt2).then_inc(mlp_in, 16)
            sp.wait_ge(dense_cleared, 2)
            for g in range(REP):
                part = slice(g * FIELDS, g * FIELDS + DENSE)
                sp.dma_start(dense_raw[part, :], dense_t).then_inc(dense_in, 16)
                sp.dma_start(wt1_d_raw[part, :], wt1[2 * P:2 * P + DENSE, :]).then_inc(dense_in, 16)

            def spread(unit, first=False):
                here, stored, made, *read = [v if first else sp.to_reg(v) for v in (
                    unit + 1, unit * 32 + 32, unit * len(PARTS), *(unit * (16 * n) for n in LOADS))]
                if not first:
                    for part in range(len(PARTS)):
                        sp.wait_ge(ab_loaded[part], read[part])
                sp.wait_ge(xt_ready, here)
                for half in range(2):
                    dst = xt_dram[half * FIELDS:(half + 1) * FIELDS, :, :]
                    sp.dma_start(bass.AP(dst.tensor, dst.offset, [[P, J], [W, FIELDS], [1, P]]),
                                 xt[:, :]).then_inc(xt_stored, 16)
                if not first:
                    sp.wait_ge(products, made)

                def bring(dst, field, turn, part):
                    src = xt_dram[field:field + FIELDS, :, :]
                    sp.dma_start(dst, bass.AP(src.tensor, src.offset, [[turn * W, REP], [W, FIELDS], [1, W]])
                                 ).then_inc(ab_loaded[part], 16)

                sp.wait_ge(xt_stored, stored)
                bring(a_rows[:, :], 0, 0, 0)
                for part, (lo_c, hi_c) in enumerate(PARTS):
                    for c in range(lo_c, hi_c):
                        bring(b_rows[:, c, :], REP * c, 0 if c == LAST else 1, part)

            spread(0, first=True)
            with sp.Fori(1, UNITS) as unit:
                spread(unit)
            sp.wait_ge(row_copied, 1)
            sp.dma_start(out.rearrange("b o -> o b"), y_row).then_inc(out_stored, 16)
            sp.wait_ge(out_stored, 16)

        @block.gpsimd
        def _(pool):
            def gather(h, ids_tile):
                pool.indirect_dma_start(
                    out=rows[:, h, :], out_offset=None, in_=tables[h],
                    in_offset=bass.IndirectOffsetOnAxis(ap=ids_tile[:, h:h + 1], axis=0)).then_inc(gathered, 16)

            pool.wait_ge(ids_in, 16)
            for h in range(FIELDS):
                gather(h, ids_all[:, 0, :])
            nc.gpsimd.memset(sums[:, 1, :, :], 0.0).then_inc(sums_done, SUMS0)

            def add_up(unit, u, pair, staged=None, tiles=2):
                if staged is not None:
                    pool.wait_ge(ids_staged, staged)
                last_step = (u * J + 2 * pair + tiles) * SPT - 1
                pool.wait_ge(scaled_done, (unit - u) * SCALED_PU + (SCALED0 + SUMS * steps_of("S", last_step)))
                first = (u % 2) * J + 2 * pair
                t = scaled[:, first:first + tiles, SUMS:ROWS, :]
                level = sum(len(x) for x in TREES[:pair])
                for n, half in TREES[pair]:
                    nc.gpsimd.tensor_tensor(t[:, :, 0:half, :], t[:, :, 0:half, :], t[:, :, n - half:n, :],
                                            ALU.add).then_inc(pool_chain, 1)
                    level += 1
                    pool.wait_ge(pool_chain, unit * LEVELS_PU + level)
                if pair == 0:
                    pool.wait_ge(finished, unit + 1)
                nc.gpsimd.tensor_tensor(sums[:, u % 2, 2 * pair:2 * pair + tiles, :], t[:, :, 0, :], t[:, :, 1, :],
                                        ALU.add).then_inc(sums_done, tiles)

            def body(t, last):
                h = 0
                for u in range(UPT):
                    unit = t * UPT + u
                    if u == 0 and not last:
                        pool.wait_ge(permuted, t * 2 + 3)
                        nc.gpsimd.tensor_copy(ids_next[:, :], ids_all[:, t + 1, :]).then_inc(ids_staged, 1)
                    for pair in range(2):
                        add_up(unit, u, pair, t + 1 if u == 0 and pair == 0 and not last else None,
                               tiles=1 if last and u == UPT - 1 and pair == 1 else 2)
                        if not last:
                            for _ in range(GATHERS[u] // 2):
                                gather(h, ids_next)
                                h += 1

            batch_tiles(pool, body)

        @block.tensor
        def _(pe):
            def transpose(unit, dg, need, first=False):
                pe.wait_ge(permuted, need)
                if not first:
                    pe.wait_ge(xt_ready, unit)
                nc.tensor.transpose(xt_ps[:, 0:P], x[:, dg, :, :], ident[:, :]).then_inc(transposed, 1)

            def layer1(unit, c, first=False):
                if c == 0 and not first:
                    pe.wait_ge(z1_added, unit)
                    pe.wait_ge(lo_done, unit)
                    pe.wait_ge(hi_done, unit)
                if c < SPLIT.start:
                    pe.wait_ge(products, unit * len(PARTS) + 1)
                    nc.tensor.matmul(cur_ps[:, :], f0[:, c, :], z[:, c, :], start=(c == 0), stop=False)
                elif c < SPLIT.stop:
                    k = c - SPLIT.start
                    pe.wait_ge(z_lo_done, unit + 1)
                    nc.tensor.matmul(cur_ps[:, :], f0_hi[:, k, :], z_hi[:, k, :], start=False, stop=False)
                    nc.tensor.matmul(cur_ps[:, :], f0_lo[:, k, :], z_hi[:, k, :], start=False, stop=False)
                    nc.tensor.matmul(cur_ps[:, :], f0_hi[:, k, :], z_lo[:, k, :], start=False, stop=False)
                else:
                    pe.wait_ge(lo5_done, unit + 1)
                    nc.tensor.matmul(cur_ps[:, :], f0p[:, :], zp[:, :], start=False, stop=True).then_inc(cur_done, 1)

            pe.wait_ge(eye_in, 16)
            transpose(0, 0, 1, first=True)
            transpose(1, 1, 2)
            pe.wait_ge(f0_split, 2)
            pe.wait_ge(f0_parted, 3)
            for c in range(CHUNKS + 1):
                layer1(0, c, first=True)
            pe.wait_ge(f1_split, 1)
            pe.wait_ge(dense_parted, 5)

            def body(t, last):
                for u in range(UPT):
                    unit = t * UPT + u
                    look, look2 = not (last and u == UPT - 1), not (last and u >= UPT - 2)
                    for q in range(STEPS):
                        j, c = q // SPT, q % SPT
                        step = u * STEPS + q
                        if look2 and q == AT_TRANSPOSE:
                            dg = (u + 2) % UPT
                            transpose(unit + 2, dg, t * 2 + (4 if u + 2 >= UPT else 2 if dg < EARLY else 3))
                        if look and q in AT_LAYER1:
                            layer1(unit + 1, AT_LAYER1.index(q))
                        if q == 0:
                            pe.wait_ge(hi_done, unit + 1)
                            pe.wait_ge(lo_done, unit + 1)
                        before = bank_before(step)
                        if OWNER[before % STEPS] == "V":
                            pe.wait_ge(macs, t * (UPT * MACS_PU) + (MAC0 + HB * steps_of("V", before)))
                        else:
                            pe.wait_ge(scaled_done, t * (UPT * SCALED_PU) + (SCALED0 + SUMS * steps_of("S", before)))
                        bank = y_ps[step % YB][:, :, :].rearrange("p h n -> p (h n)")
                        cols = slice(c * W, (c + 1) * W)
                        hi = cur_hi[:, u % 2, j * P:(j + 1) * P]
                        lo = cur_lo[:, u % 2, j * P:(j + 1) * P]
                        nc.tensor.matmul(bank, hi, f1_hi[:, cols], start=True, stop=False)
                        nc.tensor.matmul(bank, hi, f1_lo[:, cols], start=False, stop=False)
                        nc.tensor.matmul(bank, lo, f1_hi[:, cols], start=False, stop=True).then_inc(y_ready, 1)

            batch_tiles(pe, body)

            pe.wait_ge(mlp_in, 16 * 5)
            pe.wait_ge(z1_reduced, BT)
            pe.wait_ge(xt_ready, UNITS)
            def transpose_z2(part):
                lo_t, hi_t = Z2_PARTS[part]
                pe.wait_ge(z2_reduced, hi_t + 1)
                if part > 0:
                    pe.wait_ge(z2t_copied, part)
                for t in range(lo_t, hi_t):
                    last = nc.tensor.transpose(xt_ps[:, t * P:(t + 1) * P], z2_all[:, t + 1, :], ident[:, :])
                last.then_inc(z2t_ready, 1)

            transpose_z2(0)
            for m in range(MLP1 // P):
                cols = slice(m * P, (m + 1) * P)
                pe.wait_ge(macs, (BT - 1) * UPT * MACS_PU + MAC0 + HB * steps_of("V", UPT * STEPS - YB + m))
                pe.wait_ge(scaled_done, (BT - 1) * UPT * SCALED_PU + SCALED0
                           + SUMS * steps_of("S", UPT * STEPS - YB + m))
                nc.tensor.matmul(h1_ps[m], wt1_sb[:, 0, cols], z1_all[:, :], start=True, stop=False)
                nc.tensor.matmul(h1_ps[m], wt1_dp[:, cols], dense_p[:, :], start=False, stop=False)
            for part, (lo_t, hi_t) in enumerate(Z2_PARTS):
                b = slice(lo_t * P, hi_t * P)
                if part > 0:
                    transpose_z2(part)
                pe.wait_ge(z2t_copied, part + 1)
                for m in range(MLP1 // P):
                    last = nc.tensor.matmul(h1_ps[m][:, b], wt1_sb[:, 1, m * P:(m + 1) * P], z2_t[:, b],
                                            start=False, stop=(part == 1))
                    if part == 1:
                        last.then_inc(h1_ready, 1)
            pe.wait_ge(macs, MAC0 + UNITS * MACS_PU)
            pe.wait_ge(scaled_done, SCALED0 + UNITS * SCALED_PU)
            for m in range(MLP2 // P):
                for k in range(MLP1 // P):
                    pe.wait_ge(h1_done, k + 1)
                    last = nc.tensor.matmul(h2_ps[m], wt2_sb[:, k, m * P:(m + 1) * P], h1[:, k, :],
                                            start=(k == 0), stop=(k == MLP1 // P - 1))
                last.then_inc(h2_ready, 1)
            for k in range(MLP2 // P):
                pe.wait_ge(h2_done, k + 1)
                last = nc.tensor.matmul(cur_ps[0:1, :], wt3_sb[:, k:k + 1], h2[:, k, :],
                                        start=(k == 0), stop=(k == MLP2 // P - 1))
            last.then_inc(row_ready, 1)

        @block.scalar
        def _(act):
            def evacuate(unit, first=False):
                act.wait_ge(transposed, unit + 1)
                if not first:
                    act.wait_ge(xt_stored, unit * 32)
                nc.scalar.copy(xt[:, :], xt_ps[:, 0:P]).then_inc(xt_ready, 1)

            def z_high(unit):
                act.wait_ge(products, unit * len(PARTS) + (SPLIT_PART + 1))
                nc.scalar.copy(z_hi[:, :, :], z[:, SPLIT, :]).then_inc(z_hi_done, 1)

            def hi5(unit):
                act.wait_ge(products, unit * len(PARTS) + len(PARTS))
                nc.scalar.copy(zp[:, :], z[:, LAST, :]).then_inc(hi5_done, 1)

            def hi(unit, parity):
                act.wait_ge(cur_done, unit + 1)
                nc.scalar.activation(cur_hi[:, parity, :], cur_ps[:, :], ACT.Relu).then_inc(hi_done, 1)

            def permute(a, b):
                nc.scalar.copy(x[:, a:b, :, :].rearrange("p g j h -> p (g j) h"),
                               rows[:, :, a * J:b * J].rearrange("p h d -> p d h")).then_inc(permuted, 1)

            act.preload_act_table(ACT.Relu)
            act.sem_inc(scaled_done, SCALED0)
            act.wait_ge(f1_in, 16)
            nc.scalar.copy(f1_hi[:, :], f1_raw).then_inc(f1_hi_done, 1)
            act.wait_ge(gathered, 16 * FIELDS)
            permute(0, 1)
            permute(1, EARLY)
            evacuate(0, first=True)
            evacuate(1)
            z_high(0)
            hi5(0)
            hi(0, 0)

            def body(t, last):
                for u in range(UPT):
                    unit = t * UPT + u
                    look, look2 = not (last and u == UPT - 1), not (last and u >= UPT - 2)
                    for q in range(STEPS):
                        j, c = q // SPT, q % SPT
                        step = u * STEPS + q
                        if u == EARLY and not last and q == AT_PERMUTE:
                            act.wait_ge(gathered, t * (16 * FIELDS) + 2 * 16 * FIELDS)
                            act.wait_ge(macs, unit * MACS_PU + MAC0)
                            act.wait_ge(scaled_done, unit * SCALED_PU + SCALED0)
                            permute(0, EARLY)
                        if u == 0 and q == AT_PERMUTE:
                            act.wait_ge(macs, unit * MACS_PU + MAC0)
                            act.wait_ge(scaled_done, unit * SCALED_PU + SCALED0)
                            permute(EARLY, UPT)
                        if look2 and q == AT_EVACUATE:
                            evacuate(unit + 2)
                        if look and q == AT_Z_HI:
                            z_high(unit + 1)
                        if look and q == AT_HI5:
                            hi5(unit + 1)
                        if look and q == AT_HI:
                            hi(unit + 1, (u + 1) % 2)
                        if OWNER[q] != "S":
                            continue
                        if c == 0:
                            act.wait_ge(sums_done, unit * J + (j + 1))
                        act.wait_ge(y_ready, t * (UPT * STEPS) + (step + 1))
                        row = HB * OWNER[j * SPT:q].count("S")
                        for r in range(HB):
                            h = c * HB + r
                            mul = nc.scalar.mul(scaled[:, (u % 2) * J + j, row + r, :],
                                                y_ps[step % YB][:, r, :], x[:, u, j, h:h + 1])
                            if (r + 1) % (HB // SUMS) == 0:
                                mul.then_inc(scaled_done, 1)

            batch_tiles(act, body)

            for part, (lo_t, hi_t) in enumerate(Z2_PARTS):
                b = slice(lo_t * P, hi_t * P)
                act.wait_ge(z2t_ready, part + 1)
                nc.scalar.copy(z2_t[:, b], xt_ps[:, b]).then_inc(z2t_copied, 1)
            for m in range(MLP1 // P):
                act.wait_ge(h1_ready, m + 1)
                nc.scalar.activation(h1[:, m, :], h1_ps[m], ACT.Relu, bias=bt1_sb[:, m:m + 1]).then_inc(h1_done, 1)
            for m in range(MLP2 // P):
                act.wait_ge(h2_ready, m + 1)
                nc.scalar.activation(h2[:, m, :], h2_ps[m], ACT.Relu, bias=bt2_sb[:, m:m + 1]).then_inc(h2_done, 1)
            act.wait_ge(row_ready, 1)
            nc.scalar.copy(y_row, cur_ps[0:1, :]).then_inc(row_copied, 1)

        @block.vector
        def _(dve):
            def product(unit, part):
                n = 16 * LOADS[part]
                chunks = slice(*PARTS[part])
                dve.wait_ge(ab_loaded[part], unit * n + n)
                a = a_rows[:, :]
                a = bass.AP(a.tensor, a.offset, [list(a.ap[0]), [0, chunks.stop - chunks.start], [1, W]])
                nc.vector.tensor_tensor(z[:, chunks, :], a, b_rows[:, chunks, :], ALU.mult).then_inc(products, 1)

            def z_low(unit):
                dve.wait_ge(z_hi_done, unit + 1)
                nc.vector.tensor_tensor(z_lo[:, :, :], z[:, SPLIT, :], z_hi[:, :, :].bitcast(f32),
                                        ALU.subtract).then_inc(z_lo_done, 1)

            def lo5(unit):
                half = slice(P // 2, P)
                dve.wait_ge(hi5_done, unit + 1)
                nc.vector.tensor_tensor(zp[half, :], z[half, LAST, :], zp[half, :].bitcast(f32),
                                        ALU.subtract).then_inc(lo5_done, 1)

            def lo(unit, parity):
                dve.wait_ge(hi_done, unit + 1)
                nc.vector.scalar_tensor_tensor(cur_lo[:, parity, :], cur_ps[:, :], 0.0,
                                               cur_hi[:, parity, :].bitcast(f32), ALU.max,
                                               ALU.subtract).then_inc(lo_done, 1)

            def add_z1(unit, u, t):
                flat = z1[:, :, :].rearrange("p j b -> p (j b)")
                if u == 0:
                    nc.vector.tensor_scalar(flat, cur_ps[:, :], 0.0, None, ALU.max).then_inc(z1_added, 1)
                else:
                    dve.wait_ge(z1_added, unit)
                    nc.vector.scalar_tensor_tensor(flat, cur_ps[:, :], 0.0, flat,
                                                   ALU.max, ALU.add).then_inc(z1_added, 1)
                if u == UPT - 1:
                    dve.wait_ge(z1_added, unit + 1)
                    nc.vector.tensor_reduce(z1_all[:, bass.ts(t, P)], z1[:, :, :].rearrange("p j b -> p b j"),
                                            AX.X, ALU.add).then_inc(z1_reduced, 1)

            def finish(unit, parity, u, part, final=False):
                if part == 0:
                    dve.wait_ge(macs, (unit + 1) * MACS_PU + MAC0)
                    nc.vector.tensor_tensor(total[:, :, :], acc[:, parity, 0, :, :], acc[:, parity, 1, :, :],
                                            ALU.add).then_inc(finish_chain, 1)
                elif part == 1:
                    dve.wait_ge(sums_done, (unit + 1) * J + SUMS0 - (1 if final else 0))
                    if final:
                        dve.wait_ge(last_sum_done, 1)
                    dve.wait_ge(finish_chain, (unit + 1) * 2 + 1)
                    nc.vector.tensor_tensor(total[:, :, :], total[:, :, :], sums[:, parity, :, :],
                                            ALU.add).then_inc(finish_chain, 1)
                elif part == 2:
                    dve.wait_ge(finish_chain, (unit + 1) * 2 + 2)
                    if u == 0:
                        nc.vector.tensor_scalar(z2[:, :, :], total[:, :, :], 0.0, None, ALU.max).then_inc(finished, 1)
                    else:
                        dve.wait_ge(finished, (unit + 1) + FINISHED0)
                        nc.vector.scalar_tensor_tensor(z2[:, :, :], total[:, :, :], 0.0, z2[:, :, :],
                                                       ALU.max, ALU.add).then_inc(finished, 1)

            def reduce_z2(unit, slot):
                dve.wait_ge(finished, (unit + 1) + (FINISHED0 + 1))
                nc.vector.tensor_reduce(z2_all[:, slot, :], z2[:, :, :].rearrange("p j n -> p n j"),
                                        AX.X, ALU.add).then_inc(z2_reduced, 1)

            nc.vector.memset(dense_raw, 0.0).then_inc(dense_cleared, 1)
            nc.vector.memset(wt1_d_raw, 0.0).then_inc(dense_cleared, 1)
            nc.vector.memset(acc[:, 1, :, :, :], 0.0).then_inc(macs, MAC0)
            nc.vector.memset(z2[:, :, :], 0.0).then_inc(finished, FINISHED0)
            dve.wait_ge(f0_in, 48)
            nc.vector.tensor_tensor(f0[:, :, :], fa[:, :, :], fb[:, :, :], ALU.add).then_inc(f0_folded, 1)
            nc.vector.tensor_copy(f0p[:, :], f0s[:, :]).then_inc(f0_parted, 1)
            dve.wait_ge(f0_folded, 1)
            nc.vector.tensor_copy(f0[0:FIELDS, 0, :], fa[0:FIELDS, 0, :]).then_inc(f0_folded, 1)
            dve.wait_ge(f0_parted, 1)
            for g in (1, 3):
                part = slice(g * FIELDS, (g + 1) * FIELDS)
                nc.vector.tensor_tensor(f0p[part, :], f0s[part, :], f0p[part, :].bitcast(f32),
                                        ALU.subtract).then_inc(f0_parted, 1)
            dve.wait_ge(f0_folded, 2)
            nc.vector.tensor_copy(f0_hi[:, :, :], f0[:, SPLIT, :]).then_inc(f0_split, 1)
            dve.wait_ge(f0_split, 1)
            nc.vector.tensor_tensor(f0_lo[:, :, :], f0[:, SPLIT, :], f0_hi[:, :, :].bitcast(f32),
                                    ALU.subtract).then_inc(f0_split, 1)
            dve.wait_ge(f1_hi_done, 1)
            nc.vector.tensor_tensor(f1_lo[:, :], f1_raw, f1_hi[:, :].bitcast(f32), ALU.subtract).then_inc(f1_split, 1)
            dve.wait_ge(dense_in, 16 * 2 * REP)
            nc.vector.tensor_copy(dense_p[:, :], dense_raw).then_inc(dense_parted, 1)
            nc.vector.tensor_copy(wt1_dp[:, :], wt1_d_raw).then_inc(dense_parted, 1)
            dve.wait_ge(dense_parted, 2)
            for p_, raw, start, width in ((dense_p, dense_raw, 2 * FIELDS, 2 * FIELDS),
                                          (wt1_dp, wt1_d_raw, FIELDS, FIELDS),
                                          (wt1_dp, wt1_d_raw, 3 * FIELDS, FIELDS)):
                part = slice(start, start + width)
                nc.vector.tensor_tensor(p_[part, :], raw[part, :], p_[part, :].bitcast(f32),
                                        ALU.subtract).then_inc(dense_parted, 1)
            for part in range(len(PARTS)):
                product(0, part)
            z_low(0)
            lo5(0)
            lo(0, 0)
            add_z1(0, 0, 0)

            def body(t, last):
                for u in range(UPT):
                    unit = t * UPT + u
                    look, look2 = not (last and u == UPT - 1), not (last and u >= UPT - 2)
                    for q in range(STEPS):
                        j, c = q // SPT, q % SPT
                        step = u * STEPS + q
                        if q in AT_FINISH:
                            finish(unit - 1, (u + 1) % 2, (u - 1) % UPT, AT_FINISH.index(q))
                        if u == 0 and q == AT_FINISH[-1]:
                            reduce_z2(unit - 1, t)
                        if look and q in AT_PRODUCT:
                            product(unit + 1, AT_PRODUCT.index(q))
                        if look and q == AT_Z_LO:
                            z_low(unit + 1)
                        if look and q == AT_LO5:
                            lo5(unit + 1)
                        if look and q == AT_LO:
                            lo(unit + 1, (u + 1) % 2)
                        if look and q == AT_Z1:
                            add_z1(unit + 1, (u + 1) % UPT, t)
                        if q == 0:
                            dve.wait_ge(finished, unit + 1)
                        if OWNER[q] != "V":
                            continue
                        start = "V" not in OWNER[j * SPT:q]
                        if start:
                            dve.wait_ge(scaled_done, t * (UPT * SCALED_PU)
                                        + (SCALED0 + SUMS * steps_of("S", u * STEPS + j * SPT - 1) + 1))
                        dve.wait_ge(y_ready, t * (UPT * STEPS) + (step + 1))
                        for r in range(HB):
                            h = c * HB + r
                            a = acc[:, u % 2, r % SUMS, j, :]
                            begun = scaled[:, (u % 2) * J + j, r, :] if start and r < SUMS else a
                            if not (start and r < SUMS):
                                dve.wait_ge(macs, t * (UPT * MACS_PU)
                                            + (MAC0 + HB * steps_of("V", step - 1) + r - SUMS + 1))
                            nc.vector.scalar_tensor_tensor(a, y_ps[step % YB][:, r, :], x[:, u, j, h:h + 1], begun,
                                                           ALU.mult, ALU.add).then_inc(macs, 1)

            batch_tiles(dve, body)
            dve.wait_ge(scaled_done, SCALED0 + UNITS * SCALED_PU)
            last_rows = scaled[:, TR - 1, SUMS:HB * OWNERS[1].count("S"), :].rearrange("p r n -> p n r")
            nc.vector.tensor_reduce(sums[:, (UNITS - 1) % 2, J - 1, :], last_rows, AX.X,
                                    ALU.add).then_inc(last_sum_done, 1)
            for part in range(3):
                finish(UNITS - 1, (UNITS - 1) % 2, UPT - 1, part, final=True)
            reduce_z2(UNITS - 1, BT)


def kernel(**inputs):
    import numpy as _np
    import concourse.bacc as _bacc
    from concourse import mybir as _mybir
    from concourse.bass_utils import run_bass_kernel_spmd as _run

    nc = _bacc.Bacc("TRN2", target_bir_lowering=False, num_devices=1)
    arrays = {}

    def put(name, a):
        a = _np.ascontiguousarray(a)
        arrays[name] = a
        return nc.dram_tensor(name, a.shape, _mybir.dt.from_np(a.dtype), kind="ExternalInput").ap()

    i = _np.arange(FIELDS)
    s = REP * _np.arange(CHUNKS)[None, :, None] + _np.arange(REP)[:, None, None]
    k = (i[None, None, :] + s) % FIELDS
    pair_a = (i * FIELDS + k).transpose(0, 2, 1).reshape(P, CHUNKS)
    pair_b = (k * FIELDS + i).transpose(0, 2, 1).reshape(P, CHUNKS)
    pair_s = _np.tile(i * FIELDS + (i + FIELDS // 2) % FIELDS, REP)
    filter_0 = _np.asarray(inputs["L0_rec_filter_0"])[0]
    args = [
        put("ids", inputs["ids"]),
        [put(f"tbl_{h}", inputs[f"tbl_{h}"]) for h in range(FIELDS)],
        put("w1a", filter_0[pair_a]),
        put("w1b", filter_0[pair_b]),
        put("w1s", filter_0[pair_s]),
        put("f1", _np.asarray(inputs["L0_rec_filter_1"])[0]),
        put("eye", _np.eye(P, dtype=_np.float32)),
        put("dense_t", _np.asarray(inputs["dense_ctx"]).T),
        put("wt1", inputs["W_top1"]),
        put("bt1", _np.asarray(inputs["b_top1"]).reshape(MLP1 // P, P).T),
        put("wt2", inputs["W_top2"]),
        put("bt2", _np.asarray(inputs["b_top2"]).reshape(MLP2 // P, P).T),
        put("wt3", _np.asarray(inputs["W_top3"]).reshape(MLP2 // P, P).T),
    ]
    out = nc.dram_tensor("out", (BATCH, 1), _mybir.dt.float32, kind="ExternalOutput").ap()
    tower(nc, *args, out)
    r = _run(nc, [arrays], core_ids=[0])
    return r.results[0]["out"]
```
